# Optimizing a Trainium2 kernel written in Bass

```python
import numpy as np
import jax
import jax.numpy as jnp

def _softmax(x, axis=-1):
    return jax.nn.softmax(x, axis=axis)

def _gelu(x):
    return jax.nn.gelu(x, approximate=True)

def _silu(x):
    return jax.nn.silu(x)

def _sigmoid(x):
    return jax.nn.sigmoid(x)

def _layernorm(x, axis=-1, eps=1e-05):
    m = jnp.mean(x, axis=axis, keepdims=True)
    v = jnp.var(x, axis=axis, keepdims=True)
    return (x - m) / jnp.sqrt(v + eps)

def _scatter_add(tgt, idx, src, axis=0):
    return tgt.at[idx].add(src)

def _segment_sum(src, seg, n):
    return jax.ops.segment_sum(src, seg, n)
kernel_name = 'mk_hybrid_d1_jaxref_r4_5c9068'

def setup_inputs(seed: int=0):
    np.random.seed(seed)
    _w = jnp.asarray

    def _L0_attn_a_setup():
        import jax, jax.numpy as jnp
        import numpy as np
        D_MODEL = 256
        NUM_HEADS = 16
        HEAD_DIM = D_MODEL // NUM_HEADS
        key = jax.random.key(seed)
        ks = jax.random.split(key, 7)
        B, T, C = (4, 512, D_MODEL)
        s = 1.0 / np.sqrt(C)
        return {'x': jax.random.normal(ks[0], (B, T, C), dtype=jnp.float32), 'ln_gamma': jnp.ones((C,), dtype=jnp.float32), 'ln_beta': jnp.zeros((C,), dtype=jnp.float32), 'w_qkv': jax.random.normal(ks[1], (C, 3 * C), dtype=jnp.float32) * s, 'b_qkv': jnp.zeros((3 * C,), dtype=jnp.float32), 'w_out': jax.random.normal(ks[2], (C, C), dtype=jnp.float32) * s, 'b_out': jnp.zeros((C,), dtype=jnp.float32)}
    _L0_attn_a_in = _L0_attn_a_setup()

    def _L0_attn_b_setup():
        import jax, jax.numpy as jnp
        import numpy as np
        H = 256
        D = 64
        CHUNK = 128
        LR = 0.1
        GRAD_SCALE = 0.1
        MAX_GRAD_NORM = 1.0
        EPS = 1e-06
        P = 2 * D * D

        def _xavier(k, shape, gain=0.1):
            fan_out, fan_in = shape
            a = gain * np.sqrt(6.0 / (fan_in + fan_out))
            return jax.random.uniform(k, shape, jnp.float32, -a, a)

        def _causal_dwconv(x, w, b):
            T = x.shape[1]
            xp = jnp.pad(x, ((0, 0), (3, 0), (0, 0)))
            y = b
            for j in range(4):
                y = y + xp[:, j:j + T, :] * w[:, j]
            return y

        def _mem_loss(p, k_t, v_t):
            W1 = p[:D * D].reshape(D, D)
            W2 = p[D * D:].reshape(D, D)
            pred = jax.nn.silu(k_t @ W1.T) @ W2.T
            return jnp.sum((pred - v_t) ** 2)
        _grad_fn = jax.vmap(jax.vmap(jax.grad(_mem_loss), in_axes=(None, 0, 0)), in_axes=(0, 0, 0))

        def _forward(hidden, Wk, Wv, Wq, Wo, ckw, ckb, cvw, cvb, cqw, cqb, mW1, mW2, aW, ab, eW, eb, tW, tb, norm_g, gW, gb):
            B, S, _ = hidden.shape
            k = _causal_dwconv(hidden @ Wk.T, ckw, ckb)
            v = _causal_dwconv(hidden @ Wv.T, cvw, cvb)
            q = _causal_dwconv(hidden @ Wq.T, cqw, cqb)
            alpha = (jax.nn.sigmoid(hidden @ aW.T + ab) * 0.1).mean(-1)
            eta = (jax.nn.sigmoid(hidden @ eW.T + eb) * 0.9 + 0.05).mean(-1)
            theta = (jax.nn.softplus(hidden @ tW.T + tb) * LR).mean(-1)
            W_state = jnp.tile(jnp.concatenate([mW1.ravel(), mW2.ravel()])[None], (B, 1))
            S_state = jnp.zeros_like(W_state)

            def step(carry, xs):
                Sm, Wm = carry
                gt, et, tt, at = xs
                Sm = et[:, None] * Sm - tt[:, None] * gt
                Wm = (1.0 - at[:, None]) * Wm + Sm
                return ((Sm, Wm), Wm)
            outs = []
            for c0 in range(0, S, CHUNK):
                sl = slice(c0, c0 + CHUNK)
                g = _grad_fn(W_state, k[:, sl], v[:, sl]) * GRAD_SCALE
                gn = jnp.maximum(jnp.linalg.norm(g, axis=-1, keepdims=True), EPS)
                g = g * jnp.minimum(MAX_GRAD_NORM / gn, 1.0)
                g = jax.lax.stop_gradient(g)
                xs = (jnp.swapaxes(g, 0, 1), eta[:, sl].T, theta[:, sl].T, alpha[:, sl].T)
                (S_state, W_state), Wtraj = jax.lax.scan(step, (S_state, W_state), xs)
                Wtraj = jnp.swapaxes(Wtraj, 0, 1)
                T = Wtraj.shape[1]
                W1t = Wtraj[..., :D * D].reshape(B, T, D, D)
                W2t = Wtraj[..., D * D:].reshape(B, T, D, D)
                h = jax.nn.silu(jnp.einsum('btd,btod->bto', q[:, sl], W1t))
                outs.append(jnp.einsum('bto,btpo->btp', h, W2t))
            retrieved = jnp.concatenate(outs, axis=1)
            out = retrieved @ Wo.T
            out = out * jax.lax.rsqrt(jnp.mean(out * out, -1, keepdims=True) + EPS) * norm_g
            gate = hidden @ gW.T + gb
            return out * gate
        key = jax.random.key(seed)
        ks = jax.random.split(key, 24)
        B, S = (1, 256)
        return {'hidden': jax.random.normal(ks[0], (B, S, H), jnp.float32), 'Wk': _xavier(ks[1], (D, H)), 'Wv': _xavier(ks[2], (D, H)), 'Wq': _xavier(ks[3], (D, H)), 'Wo': _xavier(ks[4], (H, D)), 'ckw': jax.random.normal(ks[5], (D, 4), jnp.float32) * 0.05, 'ckb': jnp.zeros((D,), jnp.float32), 'cvw': jax.random.normal(ks[6], (D, 4), jnp.float32) * 0.05, 'cvb': jnp.zeros((D,), jnp.float32), 'cqw': jax.random.normal(ks[7], (D, 4), jnp.float32) * 0.05, 'cqb': jnp.zeros((D,), jnp.float32), 'mW1': _xavier(ks[8], (D, D)), 'mW2': _xavier(ks[9], (D, D)), 'aW': jax.random.normal(ks[10], (D, H), jnp.float32) * 0.02, 'ab': jnp.zeros((D,), jnp.float32), 'eW': jax.random.normal(ks[11], (D, H), jnp.float32) * 0.02, 'eb': jnp.zeros((D,), jnp.float32), 'tW': jax.random.normal(ks[12], (D, H), jnp.float32) * 0.02, 'tb': jnp.zeros((D,), jnp.float32), 'norm_g': jnp.ones((H,), jnp.float32), 'gW': jnp.zeros((H, H), jnp.float32), 'gb': jnp.ones((H,), jnp.float32)}
    _L0_attn_b_in = _L0_attn_b_setup()

    def _L0_ffn_setup():
        import jax, jax.numpy as jnp
        import numpy as np
        EPS = 1e-05

        @jax.custom_vjp
        def ste_quantize(w):
            scale = jnp.maximum(jnp.mean(jnp.abs(w)), EPS)
            return jnp.clip(jnp.round(w / scale), -1.0, 1.0)

        def _ste_fwd(w):
            return (ste_quantize(w), None)

        def _ste_bwd(_, g):
            return (g,)
        ste_quantize.defvjp(_ste_fwd, _ste_bwd)
        key = jax.random.key(seed)
        k1, k2 = jax.random.split(key)
        x = jax.random.normal(k1, (8, 2048, 256), dtype=jnp.float32)
        weight = jax.random.normal(k2, (256, 256), dtype=jnp.float32) * 0.02
        return {'x': x, 'weight': weight}
    _L0_ffn_in = _L0_ffn_setup()
    _d = {'L0_attn_a_x': _L0_attn_a_in['x'], 'L0_attn_a_ln_gamma': _L0_attn_a_in['ln_gamma'], 'L0_attn_a_ln_beta': _L0_attn_a_in['ln_beta'], 'L0_attn_a_w_qkv': _L0_attn_a_in['w_qkv'], 'L0_attn_a_b_qkv': _L0_attn_a_in['b_qkv'], 'L0_attn_a_w_out': _L0_attn_a_in['w_out'], 'L0_attn_a_b_out': _L0_attn_a_in['b_out'], 'L0_attn_b_Wk': _L0_attn_b_in['Wk'], 'L0_attn_b_Wv': _L0_attn_b_in['Wv'], 'L0_attn_b_Wq': _L0_attn_b_in['Wq'], 'L0_attn_b_Wo': _L0_attn_b_in['Wo'], 'L0_attn_b_ckw': _L0_attn_b_in['ckw'], 'L0_attn_b_ckb': _L0_attn_b_in['ckb'], 'L0_attn_b_cvw': _L0_attn_b_in['cvw'], 'L0_attn_b_cvb': _L0_attn_b_in['cvb'], 'L0_attn_b_cqw': _L0_attn_b_in['cqw'], 'L0_attn_b_cqb': _L0_attn_b_in['cqb'], 'L0_attn_b_mW1': _L0_attn_b_in['mW1'], 'L0_attn_b_mW2': _L0_attn_b_in['mW2'], 'L0_attn_b_aW': _L0_attn_b_in['aW'], 'L0_attn_b_ab': _L0_attn_b_in['ab'], 'L0_attn_b_eW': _L0_attn_b_in['eW'], 'L0_attn_b_eb': _L0_attn_b_in['eb'], 'L0_attn_b_tW': _L0_attn_b_in['tW'], 'L0_attn_b_tb': _L0_attn_b_in['tb'], 'L0_attn_b_norm_g': _L0_attn_b_in['norm_g'], 'L0_attn_b_gW': _L0_attn_b_in['gW'], 'L0_attn_b_gb': _L0_attn_b_in['gb'], 'L0_ffn_weight': _L0_ffn_in['weight']}
    _x0 = _d['L0_attn_a_x']
    _d['L0_attn_a_x'] = jax.random.normal(jax.random.fold_in(jax.random.key(seed), 1), (4, 1024, 256), dtype=_x0.dtype)
    del _x0
    return _d

def reference(L0_attn_a_x, L0_attn_a_ln_gamma, L0_attn_a_ln_beta, L0_attn_a_w_qkv, L0_attn_a_b_qkv, L0_attn_a_w_out, L0_attn_a_b_out, L0_attn_b_Wk, L0_attn_b_Wv, L0_attn_b_Wq, L0_attn_b_Wo, L0_attn_b_ckw, L0_attn_b_ckb, L0_attn_b_cvw, L0_attn_b_cvb, L0_attn_b_cqw, L0_attn_b_cqb, L0_attn_b_mW1, L0_attn_b_mW2, L0_attn_b_aW, L0_attn_b_ab, L0_attn_b_eW, L0_attn_b_eb, L0_attn_b_tW, L0_attn_b_tb, L0_attn_b_norm_g, L0_attn_b_gW, L0_attn_b_gb, L0_ffn_weight):

    def _L0_attn_a_ref(x, ln_gamma, ln_beta, w_qkv, b_qkv, w_out, b_out):
        import jax, jax.numpy as jnp
        import numpy as np
        D_MODEL = 256
        NUM_HEADS = 16
        HEAD_DIM = D_MODEL // NUM_HEADS
        B, T, C = x.shape
        residual = x
        mu = jnp.mean(x, axis=-1, keepdims=True)
        var = jnp.var(x, axis=-1, keepdims=True)
        h = (x - mu) * jax.lax.rsqrt(var + 1e-05) * ln_gamma + ln_beta
        qkv = (h @ w_qkv + b_qkv).reshape(B, T, 3, NUM_HEADS, HEAD_DIM)
        qkv = jnp.transpose(qkv, (2, 0, 3, 1, 4))
        q, k, v = (qkv[0], qkv[1], qkv[2])
        scores = jnp.einsum('bhqd,bhkd->bhqk', q, k) / np.sqrt(HEAD_DIM)
        attn = jax.nn.softmax(scores, axis=-1)
        out = jnp.einsum('bhqk,bhkd->bhqd', attn, v)
        out = jnp.transpose(out, (0, 2, 1, 3)).reshape(B, T, C)
        out = out @ w_out + b_out
        return residual + out

    def _L0_attn_b_ref(hidden, Wk, Wv, Wq, Wo, ckw, ckb, cvw, cvb, cqw, cqb, mW1, mW2, aW, ab, eW, eb, tW, tb, norm_g, gW, gb):
        import jax, jax.numpy as jnp
        import numpy as np
        H = 256
        D = 64
        CHUNK = 128
        LR = 0.1
        GRAD_SCALE = 0.1
        MAX_GRAD_NORM = 1.0
        EPS = 1e-06
        P = 2 * D * D

        def _xavier(k, shape, gain=0.1):
            fan_out, fan_in = shape
            a = gain * np.sqrt(6.0 / (fan_in + fan_out))
            return jax.random.uniform(k, shape, jnp.float32, -a, a)

        def _causal_dwconv(x, w, b):
            T = x.shape[1]
            xp = jnp.pad(x, ((0, 0), (3, 0), (0, 0)))
            y = b
            for j in range(4):
                y = y + xp[:, j:j + T, :] * w[:, j]
            return y

        def _mem_loss(p, k_t, v_t):
            W1 = p[:D * D].reshape(D, D)
            W2 = p[D * D:].reshape(D, D)
            pred = jax.nn.silu(k_t @ W1.T) @ W2.T
            return jnp.sum((pred - v_t) ** 2)
        _grad_fn = jax.vmap(jax.vmap(jax.grad(_mem_loss), in_axes=(None, 0, 0)), in_axes=(0, 0, 0))

        def _forward(hidden, Wk, Wv, Wq, Wo, ckw, ckb, cvw, cvb, cqw, cqb, mW1, mW2, aW, ab, eW, eb, tW, tb, norm_g, gW, gb):
            B, S, _ = hidden.shape
            k = _causal_dwconv(hidden @ Wk.T, ckw, ckb)
            v = _causal_dwconv(hidden @ Wv.T, cvw, cvb)
            q = _causal_dwconv(hidden @ Wq.T, cqw, cqb)
            alpha = (jax.nn.sigmoid(hidden @ aW.T + ab) * 0.1).mean(-1)
            eta = (jax.nn.sigmoid(hidden @ eW.T + eb) * 0.9 + 0.05).mean(-1)
            theta = (jax.nn.softplus(hidden @ tW.T + tb) * LR).mean(-1)
            W_state = jnp.tile(jnp.concatenate([mW1.ravel(), mW2.ravel()])[None], (B, 1))
            S_state = jnp.zeros_like(W_state)

            def step(carry, xs):
                Sm, Wm = carry
                gt, et, tt, at = xs
                Sm = et[:, None] * Sm - tt[:, None] * gt
                Wm = (1.0 - at[:, None]) * Wm + Sm
                return ((Sm, Wm), Wm)
            outs = []
            for c0 in range(0, S, CHUNK):
                sl = slice(c0, c0 + CHUNK)
                g = _grad_fn(W_state, k[:, sl], v[:, sl]) * GRAD_SCALE
                gn = jnp.maximum(jnp.linalg.norm(g, axis=-1, keepdims=True), EPS)
                g = g * jnp.minimum(MAX_GRAD_NORM / gn, 1.0)
                g = jax.lax.stop_gradient(g)
                xs = (jnp.swapaxes(g, 0, 1), eta[:, sl].T, theta[:, sl].T, alpha[:, sl].T)
                (S_state, W_state), Wtraj = jax.lax.scan(step, (S_state, W_state), xs)
                Wtraj = jnp.swapaxes(Wtraj, 0, 1)
                T = Wtraj.shape[1]
                W1t = Wtraj[..., :D * D].reshape(B, T, D, D)
                W2t = Wtraj[..., D * D:].reshape(B, T, D, D)
                h = jax.nn.silu(jnp.einsum('btd,btod->bto', q[:, sl], W1t))
                outs.append(jnp.einsum('bto,btpo->btp', h, W2t))
            retrieved = jnp.concatenate(outs, axis=1)
            out = retrieved @ Wo.T
            out = out * jax.lax.rsqrt(jnp.mean(out * out, -1, keepdims=True) + EPS) * norm_g
            gate = hidden @ gW.T + gb
            return out * gate
        return _forward(hidden, Wk, Wv, Wq, Wo, ckw, ckb, cvw, cvb, cqw, cqb, mW1, mW2, aW, ab, eW, eb, tW, tb, norm_g, gW, gb)

    def _L0_ffn_ref(x, weight):
        import jax, jax.numpy as jnp
        import numpy as np
        EPS = 1e-05

        @jax.custom_vjp
        def ste_quantize(w):
            scale = jnp.maximum(jnp.mean(jnp.abs(w)), EPS)
            return jnp.clip(jnp.round(w / scale), -1.0, 1.0)

        def _ste_fwd(w):
            return (ste_quantize(w), None)

        def _ste_bwd(_, g):
            return (g,)
        ste_quantize.defvjp(_ste_fwd, _ste_bwd)
        w_ternary = ste_quantize(weight)
        scale = jnp.maximum(jnp.mean(jnp.abs(weight)), EPS)
        return jnp.einsum('bsi,oi->bso', x, w_ternary * scale)
    x = L0_attn_a_x
    x = x + _L0_attn_a_ref(_layernorm(x, axis=-1), L0_attn_a_ln_gamma, L0_attn_a_ln_beta, L0_attn_a_w_qkv, L0_attn_a_b_qkv, L0_attn_a_w_out, L0_attn_a_b_out)
    x = x + _L0_ffn_ref(_layernorm(x, axis=-1), L0_ffn_weight)
    x = x + _L0_attn_b_ref(_layernorm(x, axis=-1), L0_attn_b_Wk, L0_attn_b_Wv, L0_attn_b_Wq, L0_attn_b_Wo, L0_attn_b_ckw, L0_attn_b_ckb, L0_attn_b_cvw, L0_attn_b_cvb, L0_attn_b_cqw, L0_attn_b_cqb, L0_attn_b_mW1, L0_attn_b_mW2, L0_attn_b_aW, L0_attn_b_ab, L0_attn_b_eW, L0_attn_b_eb, L0_attn_b_tW, L0_attn_b_tb, L0_attn_b_norm_g, L0_attn_b_gW, L0_attn_b_gb)
    x = x + _L0_ffn_ref(_layernorm(x, axis=-1), L0_ffn_weight)
    return x

_drawn_inputs = setup_inputs


def setup_inputs(seed=0):
    import zlib

    import numpy as np

    out = dict(_drawn_inputs(seed))
    spreads = {'L0_attn_a_ln_gamma': (1.0, 0.6),
     'L0_attn_a_ln_beta': (0.0, 0.1),
     'L0_attn_a_b_qkv': (0.0, 0.1),
     'L0_attn_a_b_out': (0.0, 0.1),
     'L0_attn_b_ckb': (0.0, 0.8),
     'L0_attn_b_cvb': (0.0, 0.8),
     'L0_attn_b_cqb': (0.0, 0.8),
     'L0_attn_b_ab': (0.0, 0.8),
     'L0_attn_b_eb': (0.0, 2.0),
     'L0_attn_b_tb': (0.0, 0.8),
     'L0_attn_b_norm_g': (1.0, 0.6),
     'L0_attn_b_gW': (0.0, 0.8),
     'L0_attn_b_gb': (1.0, 0.6)}
    factors = {'L0_attn_b_Wk': 8.0,
     'L0_attn_b_Wv': 8.0,
     'L0_attn_b_Wq': 8.0,
     'L0_attn_b_Wo': 8.0,
     'L0_attn_b_ckw': 8.0,
     'L0_attn_b_cvw': 8.0,
     'L0_attn_b_cqw': 8.0,
     'L0_attn_b_mW1': 8.0,
     'L0_attn_b_mW2': 8.0,
     'L0_attn_b_aW': 8.0,
     'L0_attn_b_eW': 8.0,
     'L0_attn_b_tW': 8.0}
    for name, (base, spread) in spreads.items():
        noise = np.random.default_rng([zlib.crc32(name.encode()), seed]).standard_normal(out[name].shape)
        drawn = base * np.exp(spread * noise) if base else spread * noise
        out[name] = jnp.asarray(drawn.astype(out[name].dtype))
    for name, factor in factors.items():
        out[name] = (out[name] * factor).astype(out[name].dtype)
    return out
```

```python
from contextlib import ExitStack

import numpy as np
import concourse.bass as bass
from concourse import mybir

ALU = mybir.AluOpType
ACT = mybir.ActivationFunctionType
AX = mybir.AxisListType
F32 = mybir.dt.float32
BF16 = mybir.dt.bfloat16

P = 128
B, T, C = 4, 1024, 256
TOK = B * T
H, HD = 16, 16
CH = C // P
CHUNK = 512
NCH = TOK // CHUNK
TPC = CHUNK // P
NT = TOK // P
LN_EPS = 1e-5
RMS_EPS = 1e-6


class Steps:

    def __init__(self, eng, sem):
        self.eng, self.sem, self.base, self.k = eng, sem, 0, 0

    def at(self, base):
        self.base, self.k = base, 0

    def did(self, ins):
        self.k += 1
        ins.then_inc(self.sem, 1)

    def settle(self):
        self.eng.wait_ge(self.sem, self.base + self.k)


COL_GAMMA, COL_BETA, COL_BQK = 0, 2, 4
COL_K, COL_Q, COL_V = 8, 13, 18
COL_GATE_B = 23
NCOLS = 26
ROW_BV, ROW_BOUT, ROW_NORMG, ROW_GB = range(4)

def retire(nc, sems):
    nc.clear_and_free_semaphores(sems)
    nc.all_engine_barrier()


def moments(dve, steps, src, stats, mv, ready, passed):
    n = src.shape[1]
    for i in range(n):
        steps.did(dve.bn_stats(stats[:, i, :], src[:, i, :]))
    steps.settle()
    dve.sem_inc(passed, 1)
    for i in range(n):
        ins = dve.bn_aggr(mv[:, i, :], stats[:, i, :])
    ins.then_inc(ready, 1)


def normalise(dve, src, mv, rstd, dst, ready):
    n = src.shape[1]
    for i in range(n):
        ins = dve.tensor_scalar(dst[:, i, :], src[:, i, :], mv[:, i, 0:1], rstd[:, i:i + 1], ALU.subtract, ALU.mult)
    ins.then_inc(ready, 1)


SCALARS = (-0.5, LN_EPS, RMS_EPS, 1.0)
S_MINUS_HALF, S_LN_EPS, S_RMS_EPS, S_ONE = range(4)


def scalar(const, which, shape):
    col = const["scalars"][:, which:which + 1]
    for _ in shape[2:]:
        col = col.unsqueeze(len(col.shape))
    return col.to_broadcast(shape)


def inverse_deviation(pool, steps, var, const, tmp, rstd, ready):
    steps.did(pool.tensor_tensor(tmp, var, scalar(const, S_LN_EPS, tmp.shape), ALU.add))
    steps.settle()
    pool.tensor_tensor(rstd, tmp, scalar(const, S_MINUS_HALF, rstd.shape), ALU.pow).then_inc(ready, 1)


def project(nc, x, w_qkv, cols, rows, const, qk_parts, v_all, xres):
    with ExitStack() as ctx:
        def sb(name, shape, dt=F32):
            return ctx.enter_context(nc.sbuf_tensor(name, shape, dt))

        sems = []
        ctx.callback(retire, nc, sems)

        def sem(name):
            sems.append(nc.alloc_semaphore("p1_" + name))
            return sems[-1]

        wq = sb("wq", [P, CH, 3 * C])
        xin = sb("xin", [P, 2, TPC, C])
        y = sb("y", [P, 2, TPC, C])
        h = sb("h", [P, 2, TPC, C])
        hT = sb("hT", [P, 2, CH, CHUNK])
        res = sb("res", [P, 2, TPC, C])
        stats = sb("stats", [P, 2, TPC, 6])
        mv, rstd = sb("mv", [P, 2, TPC, 2]), sb("rstd", [P, 2, TPC])
        tmp = sb("var_eps", [P, TPC])
        rest = sb("rest", [P, 4, CHUNK])
        parts = sb("parts", [P, 4, 3, CHUNK], BF16)
        ps_t = ctx.enter_context(nc.psum_tensor("ps_t", [P, CH, CHUNK], F32))
        ps_qk = ctx.enter_context(nc.psum_tensor("ps_qk", [P, 4, CHUNK], F32))
        ps_v = ctx.enter_context(nc.psum_tensor("ps_v", [P, 2, 2, C], F32))

        w_in, x_in = sem("weights_loaded"), [sem("x_loaded_even"), sem("x_loaded_odd")]
        y_ready, h_ready, hT_ready = sem("y_ready"), sem("h_ready"), sem("hT_ready")
        y_added, hT_turned, v_ready = sem("y_added"), sem("hT_in_psum"), sem("v_in_psum")
        qk_ready, hi_ready, rest_ready = sem("qk_in_psum"), sem("hi_ready"), sem("rest_ready")
        mid_ready, lo_ready = sem("mid_ready"), sem("lo_ready")
        parts_out = [sem(f"parts_{j}_stored") for j in range(4)]
        var_x, var_y, rstd_x, rstd_y = sem("var_x_ready"), sem("var_y_ready"), sem("rstd_x_ready"), sem("rstd_y_ready")
        v_taken, own, pool_own = sem("v_taken"), sem("vector_steps"), sem("pool_steps")
        res_ready, res_out, passed = sem("res_ready"), sem("res_stored"), sem("passed")
        xres_c = xres.rearrange("(n i p) c -> n p i c", i=TPC, p=P)
        x_c = x.rearrange("(n i p) c -> n p i c", i=TPC, p=P)
        ROUNDS = NCH // 2
        block = ctx.enter_context(nc.Block())

        @block.sync
        def _(sp):
            def load(r, s):
                sp.wait_ge(y_added, 2 * r + s)
                sp.dma_start(xin[:, s], x_c[2 * r + s]).then_inc(x_in[s], 16)

            def store(r, s):
                sp.wait_ge(res_ready, 2 * r + s + 1)
                sp.dma_start(xres_c[2 * r + s], res[:, s]).then_inc(res_out, 16)
                for j in range(4):
                    sp.wait_ge(lo_ready, 4 * (2 * r + s) + j + 1)
                    dst = qk_parts[j // 2, bass.ds(C * r + P * (j % 2), P), :, s * CHUNK:(s + 1) * CHUNK]
                    sp.dma_start(dst, parts[:, j]).then_inc(parts_out[j], 16)

            load(0, 0)
            sp.dma_start(wq[:], w_qkv.rearrange("(g p) n -> p g n", p=P)).then_inc(w_in, 16)
            load(0, 1)
            with sp.Fori(0, ROUNDS - 1) as r:
                for s in range(2):
                    load(r + 1, s)
                    store(r, s)
            for s in range(2):
                store(ROUNDS - 1, s)
            for stored in parts_out:
                sp.wait_ge(stored, 16 * NCH)
            sp.wait_ge(res_out, 16 * NCH)

        @block.vector
        def _(dve):
            steps = Steps(dve, own)

            def norm_x(r, s):
                dve.wait_ge(x_in[s], 16 * r + 16)
                moments(dve, steps, xin[:, s], stats[:, 0], mv[:, 0], var_x, passed)

            def norm_y(r, s):
                n = 2 * r + s
                dve.wait_ge(rstd_x, n + 1)
                dve.wait_ge(y_added, n)
                normalise(dve, xin[:, s], mv[:, 0], rstd[:, 0], y[:, s], y_ready)
                dve.wait_ge(y_ready, n + 1)
                moments(dve, steps, y[:, s], stats[:, 1], mv[:, 1], var_y, passed)

            def norm_h(r, s):
                n = 2 * r + s
                dve.wait_ge(rstd_y, n + 1)
                dve.wait_ge(hT_turned, n)
                normalise(dve, y[:, s], mv[:, 1], rstd[:, 1], h[:, s], h_ready)

            def rests(r, s):
                n = 2 * r + s
                for j in range(4):
                    dve.wait_ge(hi_ready, 4 * n + j + 1)
                    if j == 0:
                        dve.wait_ge(lo_ready, 4 * n)
                    dve.scalar_tensor_tensor(out=rest[:, j], in0=ps_qk[:, j], scalar=cols[:, COL_BQK + j:COL_BQK + j + 1],
                                             in1=parts[:, j, 0], op0=ALU.add, op1=ALU.subtract).then_inc(rest_ready, 1)

            def values(r, s):
                n = 2 * r + s
                for i in range(2):
                    dve.wait_ge(v_ready, 2 * n + i + 3)
                    k = TPC * s + 2 * i
                    for t in range(2):
                        ins = dve.tensor_tensor(v_all[:, bass.ds(4 * r, 4), k + t], ps_v[:, i, t].rearrange("p (g c) -> p g c", g=4),
                                                rows[:, ROW_BV].rearrange("p (g c) -> p g c", g=4), ALU.add)
                    ins.then_inc(v_taken, 1)

            def step(r, s, after):
                steps.at(2 * TPC * (2 * r + s + 2))
                if after:
                    norm_x(r + 1, s)
                rests(r, s)
                if after:
                    norm_y(r + 1, s)
                values(r, s)
                if after:
                    norm_h(r + 1, s)

            for s in range(2):
                steps.at(2 * TPC * s)
                norm_x(0, s)
                norm_y(0, s)
                norm_h(0, s)
            with dve.Fori(0, ROUNDS - 1) as r:
                for s in range(2):
                    step(r, s, True)
            for s in range(2):
                step(ROUNDS - 1, s, False)

        @block.gpsimd
        def _(pool):
            pool.sem_inc(y_added, 1)

            steps = Steps(pool, pool_own)

            def deviation(r, s, k, var_ready, ready):
                n = 2 * r + s
                pool.wait_ge(var_ready, n + 1)
                steps.at(2 * n + k)
                inverse_deviation(pool, steps, mv[:, k, :, 1], const, tmp[:], rstd[:, k], ready)

            def residual(r, s):
                n = 2 * r + s
                at = res[:, s]
                pool.wait_ge(y_ready, n + 1)
                pool.wait_ge(res_out, 16 * n)
                pool.tensor_tensor(at, xin[:, s], y[:, s], ALU.add).then_inc(y_added, 1)
                pool.wait_ge(y_added, n + 2)
                pool.tensor_tensor(at, at, rows[:, ROW_BOUT:ROW_BOUT + 1].to_broadcast([P, TPC, C]), ALU.add).then_inc(res_ready, 1)

            def lows(r, s):
                n = 2 * r + s
                for j in range(4):
                    pool.wait_ge(mid_ready, 4 * n + j + 1)
                    pool.tensor_tensor(parts[:, j, 2], rest[:, j], parts[:, j, 1], ALU.subtract).then_inc(lo_ready, 1)

            def step(r, s, after):
                if after:
                    deviation(r + 1, s, 0, var_x, rstd_x)
                lows(r, s)
                if after:
                    deviation(r + 1, s, 1, var_y, rstd_y)
                    residual(r + 1, s)

            for s in range(2):
                deviation(0, s, 0, var_x, rstd_x)
                deviation(0, s, 1, var_y, rstd_y)
                residual(0, s)
            with pool.Fori(0, ROUNDS - 1) as r:
                for s in range(2):
                    step(r, s, True)
            for s in range(2):
                step(ROUNDS - 1, s, False)

        @block.scalar
        def _(act):
            def turned(r, s):
                n = 2 * r + s
                act.wait_ge(hT_turned, n + 2)
                act.wait_ge(v_ready, 2 * n)
                for c in range(CH):
                    ins = act.activation(hT[:, s, c], ps_t[:, c], ACT.Identity, bias=cols[:, COL_BETA + c:COL_BETA + c + 1],
                                         scale=cols[:, COL_GAMMA + c:COL_GAMMA + c + 1])
                ins.then_inc(hT_ready, 1)

            def splits(r, s):
                n = 2 * r + s
                for j in range(5):
                    if j < 4:
                        act.wait_ge(qk_ready, 4 * n + j + 1)
                        act.wait_ge(parts_out[j], 16 * n)
                        act.activation(parts[:, j, 0], ps_qk[:, j], ACT.Identity,
                                       bias=cols[:, COL_BQK + j:COL_BQK + j + 1]).then_inc(hi_ready, 1)
                    if j:
                        act.wait_ge(rest_ready, 4 * n + j)
                        act.activation(parts[:, j - 1, 1], rest[:, j - 1], ACT.Identity).then_inc(mid_ready, 1)

            turned(0, 0)
            with act.Fori(0, ROUNDS - 1) as r:
                for s in range(2):
                    turned(r + s, 1 - s)
                    splits(r, s)
            turned(ROUNDS - 1, 1)
            splits(ROUNDS - 1, 0)
            splits(ROUNDS - 1, 1)

        @block.tensor
        def _(pe):
            pe.sem_inc(hT_turned, 1)
            pe.sem_inc(v_ready, 2)

            def transposes(r, s):
                n = 2 * r + s
                pe.wait_ge(h_ready, n + 1)
                pe.wait_ge(hT_ready, n)
                for c in range(CH):
                    for i in range(TPC):
                        ins = pe.transpose(ps_t[:, c, i * P:(i + 1) * P], h[:, s, i, c * P:(c + 1) * P], const["ident"][:])
                ins.then_inc(hT_turned, 1)

            def products(r, s):
                n = 2 * r + s
                pe.wait_ge(hT_ready, n + 1)
                for j in range(4):
                    pe.wait_ge(rest_ready, 4 * n)
                    for c in range(CH):
                        ins = pe.matmul(ps_qk[:, j], wq[:, c, j * P:(j + 1) * P], hT[:, s, c], start=c == 0, stop=c == CH - 1)
                    ins.then_inc(qk_ready, 1)
                for i in range(TPC):
                    if i % 2 == 0:
                        pe.wait_ge(v_taken, 2 * n)
                    for c in range(CH):
                        ins = pe.matmul(ps_v[:, i // 2, i % 2], hT[:, s, c, i * P:(i + 1) * P], wq[:, c, 2 * C:],
                                        start=c == 0, stop=c == CH - 1)
                    if i % 2:
                        ins.then_inc(v_ready, 1)

            pe.wait_ge(w_in, 16)
            transposes(0, 0)
            with pe.Fori(0, ROUNDS - 1) as r:
                for s in range(2):
                    transposes(r + s, 1 - s)
                    products(r, s)
            transposes(ROUNDS - 1, 1)
            products(ROUNDS - 1, 0)
            products(ROUNDS - 1, 1)


GH = 4
NG = B * H // GH
CG = GH * HD
QC = T // CHUNK
KT = T // P
PARTS = 3
PAIRS = 6
Q_PART = (0, 0, 1, 1, 0, 2)
K_PART = (0, 1, 0, 1, 2, 0)
MROW = PAIRS * HD
ROWS = MROW + 2
SLOTS = 3
P_RING = 3
M_RING = 3
M_MMS = GH * (CHUNK // P) * (T // CHUNK)


def sums_of(oT, batches, per_head):
    rows = slice(batches.start * NG // B * P, batches.stop * NG // B * P)
    return oT[rows].rearrange("(h r) (j t) -> r h j t", r=2 * HD, j=per_head)[HD]


def inverses_of(inverse, batches, per_head):
    return inverse[batches.start * H:batches.stop * H].rearrange("h (j t) -> h j t", j=per_head)


def attend(nc, qk_parts, v_all, oT, inverse):
    with ExitStack() as ctx:
        def sb(name, shape, dt=F32):
            return ctx.enter_context(nc.sbuf_tensor(name, shape, dt))

        def sem(name):
            return ctx.enter_context(nc.semaphore("p2_" + name))

        q_st = [sb(f"q_stack{i}", [ROWS, GH, T], BF16) for i in range(SLOTS)]
        k_st = [sb(f"k_stack{i}", [ROWS, GH, T], BF16) for i in range(SLOTS)]
        v_st = [sb(f"v_ones{i}", [P, KT, GH, 2 * HD]) for i in range(SLOTS)]
        prob = [sb(f"prob{i}", [P, GH, CHUNK]) for i in range(P_RING)]
        maxes = sb("maxes", [P, M_MMS // 2, 2])
        maxm = sb("maxm", [P, M_MMS // 2])
        neg = sb("neg_max", [P, 2, M_MMS // 2], BF16)
        negT = [sb(f"neg_maxT{i}", [P, 32], BF16) for i in range(QC)]
        o_sb = [sb(f"o_sb{i}", [P, CHUNK]) for i in range(QC)]
        ps_s = ctx.enter_context(nc.psum_tensor("ps_s", [P, 2, 2, CHUNK], F32))
        ps_m = ctx.enter_context(nc.psum_tensor("ps_m", [P, M_RING, CHUNK], F32))
        ps_o = ctx.enter_context(nc.psum_tensor("ps_o", [P, CHUNK], F32))

        stack_in = [sem(f"stack{i}_loaded") for i in range(SLOTS)]
        ones_set, v_set = sem("ones_set"), sem("v_placed")
        m_ready, m_taken, m_turned = sem("scores_for_max"), sem("max_taken"), sem("max_turned")
        m_in = [sem(f"max_rows_placed{i}") for i in range(QC)]
        m_stored = [sem(f"max_stored{i}") for i in range(QC)]
        neg_rows = nc.dram_tensor("neg_rows", (QC, 32, P), BF16).ap()
        s_ready = sem("scores_for_exp")
        exp_done, pv_done = sem("exp_done"), sem("pv_done")
        o_taken, o_out = sem("o_taken"), [sem(f"o_stored{i}") for i in range(QC)]
        own = sem("vector_steps")
        early = slice(0, B - 1)
        sums, per_head = sb("sums", [2 * H * (B - 1), CHUNK]), 2
        sums_in, inverted, inverse_out = sem("sums_loaded"), sem("inverted"), sem("inverses_stored")
        EXPS, UNITS = 2 * QC * KT, QC * KT
        block = ctx.enter_context(nc.Block())

        @block.sync
        def _(sp):
            def load(g, slot):
                for qk, stack, part in ((0, q_st, Q_PART), (1, k_st, K_PART)):
                    src = qk_parts[qk, bass.ds(g * CG, CG)].rearrange("(h d) a t -> d a h t", d=HD)
                    for i in range(PAIRS):
                        sp.dma_start(stack[slot][i * HD:(i + 1) * HD], src[:, part[i]]).then_inc(stack_in[slot], 16)

            def place_max(g, slot, qc):
                half = QC * g + qc
                sp.wait_ge(m_turned, half + 1)
                sp.dma_start(neg_rows[qc].rearrange("(a b) (c i) -> c (a b) i", a=2, c=4), negT[qc][:]).then_inc(m_stored[qc], 16)
                sp.wait_ge(m_stored[qc], 16 * g + 16)
                sp.dma_start(q_st[slot][MROW:ROWS, :, qc * CHUNK:(qc + 1) * CHUNK],
                             neg_rows[qc].rearrange("(a h t) q -> a h (t q)", a=2, h=GH)).then_inc(m_in[qc], 16)

            def store(g, qc):
                sp.wait_ge(o_taken, QC * g + qc + 1)
                sp.dma_start(oT[bass.ds(g * P, P), qc * CHUNK:(qc + 1) * CHUNK], o_sb[qc][:]).then_inc(o_out[qc], 16)

            def group(g, u, load_ahead=True, first=False, last=False):
                if load_ahead:
                    if not first:
                        sp.wait_ge(exp_done, EXPS * g + 2)
                    load(g + 2, (u + 2) % SLOTS)
                if not first:
                    store(g - 1, 1)
                if not last:
                    place_max(g + 1, (u + 1) % SLOTS, 0)
                if last:
                    sp.wait_ge(inverted, 1)
                    sp.dma_start(inverses_of(inverse, early, per_head), sums[:]).then_inc(inverse_out, 16)
                store(g, 0)
                if not last:
                    place_max(g + 1, (u + 1) % SLOTS, 1)
                else:
                    store(g, 1)

            load(0, 0)
            load(1, 1)
            place_max(0, 0, 0)
            place_max(0, 0, 1)
            for g in range(3):
                group(g, g, first=g == 0)
            with sp.Fori(1, 4) as it:
                for u in range(3):
                    group(3 * it + u, u)
            for g in range(12, NG):
                if g == NG - 3:
                    sp.wait_ge(o_out[0], 16 * g)
                    sp.wait_ge(o_out[1], 16 * (g - 1))
                    sp.dma_start(sums[:], sums_of(oT, early, per_head)).then_inc(sums_in, 16)
                group(g, g % 3, load_ahead=g + 2 < NG, last=g == NG - 1)
            for s in o_out:
                sp.wait_ge(s, 16 * NG)
            sp.wait_ge(inverse_out, 16)

        @block.gpsimd
        def _(pool):
            def place_v(g, slot, first=False):
                if not first:
                    pool.wait_ge(pv_done, UNITS * (g - 2) + 2)
                pool.tensor_copy(v_st[slot][:, :, :, 0:HD],
                                 v_all[:, bass.ds(g, 1)].rearrange("p g k (h d) -> p (g k) h d", d=HD)).then_inc(v_set, 1)

            for i in range(SLOTS):
                pool.memset(v_st[i][:, :, :, HD:], 1.0).then_inc(ones_set, 1)
                place_v(i, i, first=True)
            with pool.Fori(1, 5) as it:
                for u in range(3):
                    place_v(3 * it + u, u)
            place_v(NG - 1, 0)

        @block.scalar
        def _(act):
            act.sem_inc(exp_done, 2)

            def take_o(g, qc):
                act.wait_ge(pv_done, UNITS * g + KT * (qc + 1) + 2)
                act.wait_ge(o_out[qc], 16 * g)
                act.activation(o_sb[qc][:], ps_o[:], ACT.Copy).then_inc(o_taken, 1)

            def group(g, u, first=False):
                for qc in range(QC):
                    for kt in range(KT):
                        n = UNITS * g + KT * qc + kt
                        act.wait_ge(pv_done, n)
                        for pair in range(2):
                            act.wait_ge(s_ready, 2 * n + pair + 1)
                            act.activation(prob[(UNITS * u + KT * qc + kt) % P_RING][:, 2 * pair:2 * pair + 2], ps_s[:, pair],
                                           ACT.Exp, scale=HD ** -0.5).then_inc(exp_done, 1)
                        if kt == 0 and not (first and qc == 0):
                            take_o(g - 1 if qc == 0 else g, 1 - qc)

            for g in range(3):
                group(g, g, first=g == 0)
            with act.Fori(1, 5) as it:
                for u in range(3):
                    group(3 * it + u, u)
            group(NG - 1, 0)
            take_o(NG - 1, 1)

        @block.vector
        def _(dve):
            steps = Steps(dve, own)
            for i in range(SLOTS):
                dve.memset(k_st[i][MROW:ROWS], 1.0).then_inc(ones_set, 1)

            def maxima(g, qc):
                half = QC * g + qc
                steps.at(3 * half)
                for i in range(M_MMS):
                    dve.wait_ge(m_ready, M_MMS * half + i + 1)
                    dve.tensor_reduce(maxes[:, i // 2, i % 2:i % 2 + 1], ps_m[:, (M0 + M_MMS * qc + i) % M_RING],
                                      AX.X, ALU.max).then_inc(m_taken, 1)
                dve.wait_ge(m_taken, M_MMS * (half + 1))
                steps.did(dve.tensor_reduce(maxm[:], maxes[:], AX.X, ALU.max))
                steps.settle()
                steps.did(dve.tensor_scalar(neg[:, 0], maxm[:], -1.0, None, ALU.mult))
                steps.settle()
                steps.did(dve.scalar_tensor_tensor(out=neg[:, 1], in0=maxm[:], scalar=-1.0, in1=neg[:, 0],
                                                   op0=ALU.mult, op1=ALU.subtract))
                steps.settle()
                dve.wait_ge(m_in[qc], 16 * g)
                dve.transpose(negT[qc][:], neg[:].rearrange("p a b -> p (a b)")).then_inc(m_turned, 1)

            M0 = 0
            maxima(0, 0)
            maxima(0, 1)
            for g in range(2):
                M0 = M_MMS * QC * (g + 1)
                maxima(g + 1, 0)
                maxima(g + 1, 1)
            with dve.Fori(1, 5) as it:
                for u in range(3):
                    M0 = M_MMS * QC * u
                    maxima(3 * it + u, 0)
                    maxima(3 * it + u, 1)
            M0 = 0
            maxima(NG - 1, 0)
            maxima(NG - 1, 1)
            dve.wait_ge(sums_in, 16)
            dve.reciprocal(sums[:], sums[:]).then_inc(inverted, 1)

        @block.tensor
        def _(pe):
            pe.sem_inc(pv_done, 2)

            def score_for_max(g, slot, qc, i):
                n = M_MMS * (QC * g + qc) + i
                if not (isinstance(n, int) and n < M_RING):
                    pe.wait_ge(m_taken, n - M_RING + 1)
                h, t, kc = i // 8, i // 2 % 4, i % 2
                q0 = qc * CHUNK + t * P
                pe.matmul(ps_m[:, (M_MMS * (QC * slot + qc) + i) % M_RING], q_st[slot][0:MROW, h, q0:q0 + P],
                          k_st[slot][0:MROW, h, kc * CHUNK:(kc + 1) * CHUNK], start=True, stop=True).then_inc(m_ready, 1)

            def scores(g, slot, qc, kt, pair):
                n = UNITS * g + KT * qc + kt
                pe.wait_ge(exp_done, 2 * n + pair + 1)
                for j in range(2):
                    h = 2 * pair + j
                    ins = pe.matmul(ps_s[:, pair, j], k_st[slot][:, h, kt * P:(kt + 1) * P],
                                    q_st[slot][:, h, qc * CHUNK:(qc + 1) * CHUNK], start=True, stop=True)
                ins.then_inc(s_ready, 1)

            def weigh(g, slot, qc, kt):
                n = UNITS * g + KT * qc + kt
                pe.wait_ge(exp_done, 2 * n + 4)
                if kt == 0:
                    pe.wait_ge(o_taken, QC * g + qc)
                    pe.wait_ge(v_set, g + 1)
                for h in range(GH):
                    ins = pe.matmul(ps_o[32 * h:32 * h + 32], v_st[slot][:, kt, h], prob[(UNITS * slot + KT * qc + kt) % P_RING][:, h],
                                    start=kt == 0, stop=kt == KT - 1)
                ins.then_inc(pv_done, 1)

            def group(g, u, ahead=True, first=False):
                nxt = (u + 1) % SLOTS
                if ahead:
                    pe.wait_ge(stack_in[nxt], 16 * 2 * PAIRS * ((g + 1 - nxt) // 3 + 1))
                for qc in range(QC):
                    pe.wait_ge(m_in[qc], 16 * (g + 1))
                    for kt in range(KT):
                        scores(g, u, qc, kt, 0)
                        if ahead:
                            for i in range(2):
                                score_for_max(g + 1, nxt, qc, 4 * kt + i)
                        scores(g, u, qc, kt, 1)
                        if ahead:
                            for i in range(2, 4):
                                score_for_max(g + 1, nxt, qc, 4 * kt + i)
                        if kt:
                            weigh(g, u, qc, kt - 1)
                        elif qc:
                            weigh(g, u, 0, KT - 1)
                        elif not first:
                            weigh(g - 1, (u - 1) % SLOTS, QC - 1, KT - 1)

            pe.wait_ge(ones_set, 2 * SLOTS)
            pe.wait_ge(stack_in[0], 16 * 2 * PAIRS)
            for qc in range(QC):
                for i in range(M_MMS):
                    score_for_max(0, 0, qc, i)
            for g in range(3):
                group(g, g, first=g == 0)
            with pe.Fori(1, 5) as it:
                for u in range(3):
                    group(3 * it + u, u)
            group(NG - 1, 0, ahead=False)
            weigh(NG - 1, 0, QC - 1, KT - 1)


HALF = 64
LO, HI = slice(0, HALF), slice(HALF, P)
MC = 128
NM = T // MC
SMALL_C, SMALL_E, SMALL_AB, SMALL_F, SMALL_THETA, SMALL_K2 = range(6)
HALO = 3


def mix(nc, const, cols, w, oT, inverse, xres, x2, hidT_out, mem):
    with ExitStack() as ctx:
        def sb(name, shape, dt=F32):
            return ctx.enter_context(nc.sbuf_tensor("p3_" + name, shape, dt))

        def sem(name):
            return ctx.enter_context(nc.semaphore("p3_" + name))

        w_out, w_t, w_p = sb("w_out", [P, CH, C]), const["ternary"], sb("w_p", [P, CH, 3 * P])
        o = [sb(f"o{s}", [P, CH, CHUNK]) for s in range(2)]
        inv = [sb(f"inverse_sums{s}", [P, CH, CHUNK]) for s in range(2)]
        x_in_t, x1_t, x2_t = ([sb(f"{k}{s}", [P, TPC, C]) for s in range(2)] for k in ("x_in", "x1", "x2"))
        z, hid, zT = sb("z", [P, TPC, C]), sb("hid", [P, TPC, C]), sb("zT", [P, CH, CHUNK])
        hT = [sb(f"hT{s}", [P, CH, CHUNK]) for s in range(2)]
        stats, mv, rstd, tmp = sb("stats", [P, 2, TPC, 6]), sb("mv", [P, 2, TPC, 2]), sb("rstd", [P, 2, TPC]), sb("tmp", [P, TPC])
        pre = [[sb(f"pre_{k}{s}", [HALF, HALO + CHUNK]) for s in range(2)] for k in "kqv"]
        k_c, v_c, q_c = ([sb(f"{k}_c{s}", [P if k == "q" else HALF, CHUNK]) for s in range(2)] for k in "kvq")
        sig_e, sig_a, sig_t, relu_t, soft = (sb(n, [P, CHUNK]) for n in ("sig_e", "sig_a", "sig_t", "relu_t", "soft"))
        eta, keep = sb("eta", [P, CHUNK]), sb("keep", [P, CHUNK])
        E, fz, kT = sb("E", [P, TPC, MC]), sb("fz", [P, TPC, MC]), sb("kT", [P, TPC, HALF])
        squares = sb("squares", [P, TPC, HALF])
        ab, C_, G, aqb = ([sb(f"{k}{s}", [P, CHUNK]) for s in range(2)] for k in ("ab", "C", "G", "aqb"))
        kce, vT = [sb(f"kce{s}", [P, TPC, P]) for s in range(2)], [sb(f"vT{s}", [P, TPC, HALF]) for s in range(2)]
        small = [sb(f"small{s}", [P, TPC, 6]) for s in range(2)]
        ps_a = ctx.enter_context(nc.psum_tensor("p3_a", [P, 2, 2, C], F32))
        ps_t = ctx.enter_context(nc.psum_tensor("p3_t", [P, CH, CHUNK], F32))
        ps_p = ctx.enter_context(nc.psum_tensor("p3_p", [P, 4, CHUNK], F32))

        w_in, o_in, x_in = sem("weights"), [sem("o0"), sem("o1")], [sem("x0"), sem("x1")]
        o_div, w_ready, var_z, rstd_z, z_ready, zT_turned, zT_ready, f_ready = map(sem, (
            "o_divided", "w_out_in_psum", "var_z", "rstd_z", "z", "zT_in_psum", "zT", "ffn_in_psum"))
        var_h, rstd_h, h_ready, hT_turned, hT_ready = map(sem, ("var_h", "rstd_h", "hid", "hidT_in_psum", "hidT"))
        x2_out, hT_out = [sem("x2_stored0"), sem("x2_stored1")], [sem("hidT_stored0"), sem("hidT_stored1")]
        p_ready, acts, act_own, conv, soft_ready, mean_ready, gate_ready, th_ready, th_taken, kv_ready, kv_taken = map(sem, (
            "projections_in_psum", "projection_banks_read", "activations_steps", "convolved", "softplus", "gate_means_in_psum",
            "gates", "theta_in_psum", "theta_taken", "kvT_in_psum", "kvT_taken"))
        kq_ready, g_ready, scanned, pool_own, fz_set, halo_set, pre_ready = map(sem, (
            "kq_in_psum", "G", "scans", "pool_steps", "zeros_set", "halos_set", "oldest_taps"))
        added_w, added_f, own_z, own_h, own_c, own_s, own_k = map(sem, (
            "added_to_x1", "added_to_x2", "stats_z_steps", "stats_h_steps", "convolution_steps", "scan_steps", "k_norms"))
        late, per_head = slice(B - 1, B), P // H
        late_sums = sb("late_sums", [P, T // per_head])
        sums_moved, inverted = sem("sums_moved"), sem("inverted")
        q_dup = [sem("q_doubled0"), sem("q_doubled1")]
        mem_done = sem("pool_memory_terms")
        ln_ready = sem("ln_ready")
        passed, terms_out, TERMS = sem("passed"), [sem("terms_stored0"), sem("terms_stored1")], 16 * 9
        ROUNDS = NCH // 2
        tok = lambda a: a.rearrange("(n i p) c -> n p i c", i=TPC, p=P)
        block = ctx.enter_context(nc.Block())

        @block.sync
        def _(sp):
            def load(r, s, first=False):
                n = 2 * r + s
                if not first:
                    sp.wait_ge(added_w, 2 * n - 2)
                for c in range(CH):
                    heads = oT[bass.ds((NG // B * r + 2 * c) * P, 2 * P), s * CHUNK:(s + 1) * CHUNK].rearrange(
                        "(h two d) t -> two h d t", two=2, d=HD)[0]
                    sp.dma_start(o[s][:, c], heads).then_inc(o_in[s], 16)
                    sums_c = inverse[bass.ds(H * r + H // CH * c, H // CH), s * CHUNK:(s + 1) * CHUNK]
                    sp.dma_start(inv[s][:, c], sums_c.unsqueeze(1).to_broadcast([H // CH, HD, CHUNK])).then_inc(o_in[s], 16)
                sp.dma_start(x_in_t[s][:], tok(xres)[2 * r + s]).then_inc(x_in[s], 16)

            def store_x2(r, s):
                sp.wait_ge(added_f, 2 * (2 * r + s) + 2)
                sp.dma_start(tok(x2)[2 * r + s], x2_t[s][:]).then_inc(x2_out[s], 16)

            def store_hT(r, s):
                sp.wait_ge(hT_ready, 2 * r + s + 1)
                sp.dma_start(hidT_out[r, :, :, s * CHUNK:(s + 1) * CHUNK], hT[s][:]).then_inc(hT_out[s], 16)

            def store_terms(r, s):
                n = 2 * r + s
                at, tiles = bass.ds(CHUNK * n, CHUNK), bass.ds(TPC * n, TPC)
                sp.wait_ge(conv, 3 * n + 3)
                sp.dma_start(q_c[s][HI], q_c[s][LO]).then_inc(q_dup[s], 16)
                sp.dma_start(mem["kv"][LO, at], k_c[s][:]).then_inc(terms_out[s], 16)
                sp.dma_start(mem["kv"][HI, at], v_c[s][:]).then_inc(terms_out[s], 16)
                sp.wait_ge(g_ready, n + 1)
                for name, tile in (("ab", ab), ("C", C_), ("G", G)):
                    sp.dma_start(mem[name][:, at], tile[s][:]).then_inc(terms_out[s], 16)
                sp.wait_ge(own_k, TPC * n + TPC)
                sp.dma_start(mem["small"][:, tiles], small[s][:]).then_inc(terms_out[s], 16)
                sp.wait_ge(mem_done, n + 1)
                for name, tile in (("vT", vT), ("kce", kce)):
                    sp.dma_start(mem[name][:, tiles], tile[s][:]).then_inc(terms_out[s], 16)
                sp.dma_start(mem["aqb"][:, at], aqb[s][:]).then_inc(terms_out[s], 16)

            load(0, 0, first=True)
            sp.dma_start(w_out[:], w["w_out"].rearrange("(g p) n -> p g n", p=P)).then_inc(w_in, 16)
            load(0, 1, first=True)
            sp.dma_start(w_p[:], w["w_p"].rearrange("(g p) n -> p g n", p=P)).then_inc(w_in, 16)
            sp.dma_start(late_sums[:], sums_of(oT, late, per_head)).then_inc(sums_moved, 16)
            store_x2(0, 0)
            sp.wait_ge(inverted, 1)
            sp.dma_start(inverses_of(inverse, late, per_head), late_sums[:]).then_inc(sums_moved, 16)
            store_hT(0, 0)
            sp.wait_ge(sums_moved, 32)
            with sp.Fori(0, ROUNDS - 1) as r:
                for s in range(2):
                    load(r + 1, s)
                    store_x2(r + s, 1 - s)
                    store_hT(r + s, 1 - s)
                    store_terms(r, s)
            store_x2(ROUNDS - 1, 1)
            store_hT(ROUNDS - 1, 1)
            store_terms(ROUNDS - 1, 0)
            store_terms(ROUNDS - 1, 1)
            for s in range(2):
                sp.wait_ge(x2_out[s], 16 * ROUNDS)
                sp.wait_ge(hT_out[s], 16 * ROUNDS)
                sp.wait_ge(terms_out[s], TERMS * ROUNDS)

        @block.gpsimd
        def _(pool):
            steps = Steps(pool, pool_own)
            pool.memset(fz[LO], 0.0).then_inc(fz_set, 1)
            pool.wait_ge(fz_set, 1)

            def deviation(r, s, k, var_ready, ready):
                n = 2 * r + s
                pool.wait_ge(var_ready, n + 1)
                steps.at(2 * n + k)
                inverse_deviation(pool, steps, mv[:, k, :, 1], const, tmp[:], rstd[:, k], ready)

            def divide(r, s):
                pool.wait_ge(o_in[s], 16 * 2 * CH * (r + 1))
                pool.tensor_tensor(o[s][:], o[s][:], inv[s][:], ALU.mult).then_inc(o_div, 1)

            def softplus(r, s, z_ahead, h_ahead):
                n = 2 * r + s
                pool.wait_ge(ln_ready, n + 1)
                pool.wait_ge(th_ready, n)
                pool.wait_ge(mem_done, n)
                pool.wait_ge(rstd_z, n + 1 + z_ahead)
                pool.wait_ge(rstd_h, n + 1 + h_ahead)
                pool.tensor_tensor(soft[HI], relu_t[HI], sig_t[HI], ALU.subtract).then_inc(soft_ready, 1)
                pool.wait_ge(soft_ready, n + 1)

            def memory_terms(r, s):
                n = 2 * r + s
                tiles = bass.ds(TPC * n, TPC)
                pool.wait_ge(scanned, n + 1)
                pool.wait_ge(q_dup[s], 16 * r + 16)
                pool.tensor_tensor(aqb[s][:], ab[s][:], q_c[s][:], ALU.mult)
                pool.wait_ge(kv_taken, n + 1)
                for j in range(2):
                    last = small[s][:, :, j:j + 1].to_broadcast([P, TPC, HALF])
                    ins = pool.tensor_tensor(kce[s][:, :, j * HALF:(j + 1) * HALF], kT[:], last, ALU.mult)
                ins.then_inc(mem_done, 1)

            def step(r, s, z_ahead=2, h_ahead=1):
                if z_ahead > 1:
                    divide(r + 1, s)
                if h_ahead:
                    deviation(r + s, 1 - s, 1, var_h, rstd_h)
                if z_ahead > 1:
                    deviation(r + 1, s, 0, var_z, rstd_z)
                softplus(r, s, z_ahead, h_ahead)
                memory_terms(r, s)

            divide(0, 0)
            divide(0, 1)
            deviation(0, 0, 0, var_z, rstd_z)
            deviation(0, 0, 1, var_h, rstd_h)
            deviation(0, 1, 0, var_z, rstd_z)
            with pool.Fori(0, ROUNDS - 1) as r:
                for s in range(2):
                    step(r, s)
            step(ROUNDS - 1, 0, z_ahead=1)
            step(ROUNDS - 1, 1, z_ahead=0, h_ahead=0)
            pool.wait_ge(mem_done, NCH)

        @block.scalar
        def _(act):
            for k in range(3):
                act.activation(pre[k][0][:, 0:HALO], cols[LO, 0:HALO], ACT.Copy, scale=0.0).then_inc(halo_set, 1)

            def copy_zT(r, s):
                act.wait_ge(zT_turned, 2 * r + s + 1)
                act.activation(zT[:], ps_t[:], ACT.Copy).then_inc(zT_ready, 1)

            def copy_hT(r, s):
                n = 2 * r + s
                act.wait_ge(hT_turned, n + 1)
                act.wait_ge(hT_out[s], 16 * r)
                act.activation(hT[s][:], ps_t[:], ACT.Copy).then_inc(hT_ready, 1)

            def gates(r, s):
                n = 2 * r + s
                base = 12 * n

                def bias(j):
                    return cols[HI, COL_GATE_B + j:COL_GATE_B + j + 1]

                act.wait_ge(soft_ready, n)
                act.wait_ge(terms_out[s], TERMS * r)
                for j, (k, dst) in enumerate(((0, sig_e), (1, sig_t), (2, sig_a))):
                    act.wait_ge(p_ready, 3 * n + j + 1)
                    act.activation(pre[k][s][:, HALO:], ps_p[LO, j], ACT.Copy).then_inc(act_own, 1)
                    if j == 1:
                        act.activation(relu_t[HI], ps_p[HI, 1], ACT.Relu, bias=bias(1))
                        act.activation(dst[HI], ps_p[HI, 1], ACT.Abs, bias=bias(1)).then_inc(acts, 1)
                    else:
                        act.activation(dst[HI], ps_p[HI, j], ACT.Sigmoid, bias=bias(j)).then_inc(acts, 1)
                act.wait_ge(acts, 3 * n + 3)
                act.activation(sig_t[HI], sig_t[HI], ACT.Sigmoid).then_inc(act_own, 1)
                if s:
                    for k in range(3):
                        ins = act.activation(pre[k][1][:, 0:HALO], pre[k][0][:, CHUNK:], ACT.Copy)
                    ins.then_inc(act_own, 1)
                act.wait_ge(act_own, (9 * r + 4) + (5 if s else 0))
                for k, dst, col in ((0, k_c, COL_K), (1, q_c, COL_Q), (2, v_c, COL_V)):
                    act.activation(dst[s][LO], pre[k][s][:, 0:CHUNK], ACT.Identity, bias=cols[LO, col + 4:col + 5],
                                   scale=cols[LO, col:col + 1]).then_inc(pre_ready, 1)
                act.activation(sig_t[HI], sig_t[HI], ACT.Ln).then_inc(ln_ready, 1)
                act.wait_ge(scanned, n)
                act.wait_ge(mean_ready, 2 * n + 1)
                act.activation(eta[:], ps_p[:, 0], ACT.Copy, scale=0.9, bias=0.05).then_inc(gate_ready, 1)
                act.wait_ge(mean_ready, 2 * n + 2)
                act.activation(keep[:], ps_p[:, 1], ACT.Copy, scale=-0.1, bias=1.0).then_inc(gate_ready, 1)

            def tails(r, s):
                n = 2 * r + s
                act.wait_ge(th_ready, n + 1)
                act.activation(small[s][:, :, SMALL_THETA], ps_p[:, 3, 0:TPC], ACT.Copy, scale=0.02).then_inc(th_taken, 1)
                act.wait_ge(kv_ready, n + 1)
                act.wait_ge(mem_done, n)
                act.wait_ge(own_k, TPC * n)
                kv = ps_p[:, 3].rearrange("p (k i d) -> p k i d", k=2, d=HALF)
                act.activation(vT[s][:], kv[:, 1], ACT.Copy)
                act.activation(kT[:], kv[:, 0], ACT.Copy).then_inc(kv_taken, 1)

            copy_zT(0, 0)
            copy_hT(0, 0)
            copy_zT(0, 1)
            with act.Fori(0, ROUNDS - 1) as r:
                for s in range(2):
                    gates(r, s)
                    copy_hT(r + s, 1 - s)
                    tails(r, s)
                    copy_zT(r + 1, s)
            gates(ROUNDS - 1, 0)
            copy_hT(ROUNDS - 1, 1)
            tails(ROUNDS - 1, 0)
            gates(ROUNDS - 1, 1)
            tails(ROUNDS - 1, 1)
            act.wait_ge(kv_taken, NCH)

        @block.vector
        def _(dve):
            norm_steps = [Steps(dve, own_z), Steps(dve, own_h)]
            conv_steps, scan_steps = Steps(dve, own_c), Steps(dve, own_s)

            def norm_z(r, s):
                n = 2 * r + s
                dve.wait_ge(x_in[s], 16 * (r + 1))
                for k in range(2):
                    dve.wait_ge(w_ready, 2 * n + k + 1)
                    dve.tensor_tensor(x1_t[s][:, 2 * k:2 * k + 2], x_in_t[s][:, 2 * k:2 * k + 2], ps_a[:, k], ALU.add).then_inc(added_w, 1)
                dve.wait_ge(added_w, 2 * n + 2)
                norm_steps[0].at(TPC * n)
                moments(dve, norm_steps[0], x1_t[s], stats[:, 0], mv[:, 0], var_z, passed)

            def put_z(r, s):
                n = 2 * r + s
                dve.wait_ge(rstd_z, n + 1)
                dve.wait_ge(zT_turned, n)
                normalise(dve, x1_t[s], mv[:, 0], rstd[:, 0], z, z_ready)

            def norm_h(r, s):
                n = 2 * r + s
                dve.wait_ge(x2_out[s], 16 * r)
                for k in range(2):
                    dve.wait_ge(f_ready, 2 * n + k + 1)
                    dve.tensor_tensor(x2_t[s][:, 2 * k:2 * k + 2], x1_t[s][:, 2 * k:2 * k + 2], ps_a[:, k], ALU.add).then_inc(added_f, 1)
                dve.wait_ge(added_f, 2 * n + 2)
                norm_steps[1].at(TPC * n)
                moments(dve, norm_steps[1], x2_t[s], stats[:, 1], mv[:, 1], var_h, passed)

            def put_h(r, s):
                n = 2 * r + s
                dve.wait_ge(rstd_h, n + 1)
                dve.wait_ge(hT_turned, n)
                normalise(dve, x2_t[s], mv[:, 1], rstd[:, 1], hid, h_ready)

            def convolve(r, s, taps):
                n = 2 * r + s
                conv_steps.at(6 * n + (3 if taps[0] > 1 else 0))
                if taps[0] == 1:
                    dve.wait_ge(pre_ready, 3 * n + 3)
                else:
                    dve.wait_ge(own_c, 6 * n + 3)
                for j in taps:
                    for k, dst, col in ((0, k_c, COL_K), (1, q_c, COL_Q), (2, v_c, COL_V)):
                        ins = dve.scalar_tensor_tensor(out=dst[s][LO], in0=pre[k][s][:, j:j + CHUNK], scalar=cols[LO, col + j:col + j + 1],
                                                       in1=dst[s][LO], op0=ALU.mult, op1=ALU.add)
                        if j < 3:
                            conv_steps.did(ins)
                        else:
                            ins.then_inc(conv, 1)
                    if j == 2:
                        conv_steps.settle()

            def scans(r, s):
                n = 2 * r + s
                scan_steps.at(2 * n)
                dve.wait_ge(gate_ready, 2 * n + 2)
                dve.wait_ge(mem_done, n)
                for i in range(TPC):
                    c = slice(i * MC, (i + 1) * MC)
                    dve.tensor_tensor_scan(fz[HI, i], eta[HI, c], const["zeros"][HI], 1.0, ALU.mult, ALU.add)
                    ins = dve.tensor_tensor_scan(E[:, i], eta[:, c], const["minus_ident"][:], 0.0, ALU.mult, ALU.add)
                scan_steps.did(ins)
                scan_steps.settle()
                for i in range(TPC):
                    c = slice(i * MC, (i + 1) * MC)
                    dve.tensor_tensor_scan(ab[s][:, c], keep[:, c], fz[:, i], const["ab_init"][:, 0:1],
                                           ALU.mult, ALU.add)
                    ins = dve.tensor_tensor_scan(C_[s][:, c], keep[:, c], E[:, i], 0.0, ALU.mult, ALU.add)
                scan_steps.did(ins)
                scan_steps.settle()
                tiles = bass.ds(TPC * n, TPC)
                c_v = C_[s].rearrange("p (i t) -> p i t", t=MC)
                ab_v = ab[s].rearrange("p (i t) -> p i t", t=MC)
                dve.tensor_copy(small[s][:, :, 0:1], c_v[:, :, MC - 1:])
                dve.tensor_copy(small[s][:, :, 1:2], E[:, :, MC - 1:])
                dve.tensor_copy(small[s][:, :, 2:3], ab_v[:, :, MC - 1:])
                dve.tensor_copy(small[s][:, :, 3:4], fz[:, :, MC - 1:]).then_inc(scanned, 1)
                dve.wait_ge(kq_ready, n + 1)
                dve.tensor_tensor(G[s][:], ps_p[:, 2], C_[s][:], ALU.mult).then_inc(g_ready, 1)
                dve.wait_ge(kv_taken, n + 1)
                dve.wait_ge(own_k, TPC * n)
                for i in range(TPC):
                    ins = dve.tensor_tensor_reduce(squares[:, i], kT[:, i], kT[:, i], 1.0, 0.0, ALU.mult, ALU.add,
                                                   small[s][:, i, SMALL_K2:SMALL_K2 + 1])
                    ins.then_inc(own_k, 1)

            dve.wait_ge(fz_set, 1)
            dve.wait_ge(halo_set, 3)
            def step(r, s, z_ahead=True, h_ahead=True):
                if h_ahead:
                    norm_h(r + s, 1 - s)
                convolve(r, s, (1,))
                if h_ahead:
                    put_h(r + s, 1 - s)
                if z_ahead:
                    norm_z(r + 1, s)
                convolve(r, s, (2, 3))
                if z_ahead:
                    put_z(r + 1, s)
                scans(r, s)

            norm_z(0, 0)
            put_z(0, 0)
            norm_h(0, 0)
            put_h(0, 0)
            dve.wait_ge(sums_moved, 16)
            dve.reciprocal(late_sums[:], late_sums[:]).then_inc(inverted, 1)
            norm_z(0, 1)
            put_z(0, 1)
            with dve.Fori(0, ROUNDS - 1) as r:
                for s in range(2):
                    step(r, s)
            step(ROUNDS - 1, 0, z_ahead=False)
            step(ROUNDS - 1, 1, z_ahead=False, h_ahead=False)
            dve.wait_ge(own_k, TPC * NCH)

        @block.tensor
        def _(pe):
            ident = const["ident"]

            def out_products(r, s):
                n = 2 * r + s
                pe.wait_ge(o_div, n + 1)
                pe.wait_ge(added_f, 2 * n)
                token_products(o[s], w_out, w_ready)

            def token_products(src, weights, done):
                for i in range(TPC):
                    for c in range(CH):
                        ins = pe.matmul(ps_a[:, i // 2, i % 2], src[:, c, i * P:(i + 1) * P], weights[:, c], start=c == 0, stop=c == CH - 1)
                    if i % 2:
                        ins.then_inc(done, 1)

            def turn(src, done):
                for c in range(CH):
                    for i in range(TPC):
                        ins = pe.transpose(ps_t[:, c, i * P:(i + 1) * P], src[:, i, c * P:(c + 1) * P], ident[:])
                ins.then_inc(done, 1)

            def turn_z(r, s):
                n = 2 * r + s
                pe.wait_ge(z_ready, n + 1)
                pe.wait_ge(hT_ready, n)
                turn(z, zT_turned)

            def ffn_products(r, s):
                n = 2 * r + s
                pe.wait_ge(zT_ready, n + 1)
                pe.wait_ge(added_w, 2 * n + 2)
                token_products(zT, w_t, f_ready)

            def turn_h(r, s):
                n = 2 * r + s
                pe.wait_ge(h_ready, n + 1)
                pe.wait_ge(zT_ready, n + 1)
                turn(hid, hT_turned)

            def projections(r, s):
                n = 2 * r + s
                pe.wait_ge(hT_ready, n + 1)
                pe.wait_ge(gate_ready, 2 * n)
                pe.wait_ge(g_ready, n)
                for j in range(3):
                    for c in range(CH):
                        ins = pe.matmul(ps_p[:, j], w_p[:, c, j * P:(j + 1) * P], hT[s][:, c], start=c == 0, stop=c == CH - 1)
                    ins.then_inc(p_ready, 1)

            def gate_means(r, s):
                n = 2 * r + s
                pe.wait_ge(acts, 3 * n + 3)
                for j, sig in enumerate((sig_e, sig_a)):
                    pe.matmul(ps_p[:, j], const["mean"][HI], sig[HI], start=True, stop=True).then_inc(mean_ready, 1)

            def memory_products(r, s):
                n = 2 * r + s
                pe.wait_ge(soft_ready, n + 1)
                pe.wait_ge(kv_taken, n)
                for i in range(TPC):
                    ins = pe.matmul(ps_p[:, 3, i:i + 1], soft[HI, i * P:(i + 1) * P], const["mean"][HI, 0:1], start=True, stop=True)
                ins.then_inc(th_ready, 1)
                pe.wait_ge(th_taken, n + 1)
                pe.wait_ge(conv, 3 * n + 3)
                for i in range(TPC):
                    c = slice(i * P, (i + 1) * P)
                    ins = pe.matmul(ps_p[:, 2, c], k_c[s][:, c], q_c[s][LO, c], start=True, stop=True)
                ins.then_inc(kq_ready, 1)
                for k, src in enumerate((k_c[s], v_c[s])):
                    for i in range(TPC):
                        ins = pe.transpose(ps_p[:, 3, (k * TPC + i) * HALF:(k * TPC + i + 1) * HALF], src[:, i * P:(i + 1) * P],
                                           ident[LO, 0:HALF])
                ins.then_inc(kv_ready, 1)

            def step(r, s, z_ahead=True, h_ahead=True):
                projections(r, s)
                if h_ahead:
                    ffn_products(r + s, 1 - s)
                if z_ahead:
                    out_products(r + 1, s)
                gate_means(r, s)
                if h_ahead:
                    turn_h(r + s, 1 - s)
                memory_products(r, s)
                if z_ahead:
                    turn_z(r + 1, s)

            pe.wait_ge(w_in, 32)
            out_products(0, 0)
            turn_z(0, 0)
            ffn_products(0, 0)
            turn_h(0, 0)
            out_products(0, 1)
            turn_z(0, 1)
            with pe.Fori(0, ROUNDS - 1) as r:
                for s in range(2):
                    step(r, s)
            step(ROUNDS - 1, 0, z_ahead=False)
            step(ROUNDS - 1, 1, z_ahead=False, h_ahead=False)


def constants(nc, const, cols, rows, w):
    with ExitStack() as ctx:
        def sb(name, shape, dt=F32):
            return ctx.enter_context(nc.sbuf_tensor("p0_" + name, shape, dt))

        sems = []
        ctx.callback(retire, nc, sems)

        def sem(name):
            sems.append(nc.alloc_semaphore("p0_" + name))
            return sems[-1]

        wt, size, small, ones = sb("wt", [P, CH, C]), sb("size", [P, CH, C]), sb("small", [P, 8]), sb("ones", [P, P])
        ps = ctx.enter_context(nc.psum_tensor("p0_ps", [P, 1], F32))
        vec_in, w_in, made, row_sums, total, own = map(sem, ("vectors", "weight", "pool_steps", "row_sums", "total", "vector_steps"))
        block = ctx.enter_context(nc.Block())

        @block.sync
        def _(sp):
            sp.dma_start(wt[:], w["w_ffn"].rearrange("(g p) n -> p g n", p=P)).then_inc(w_in, 16)
            sp.dma_start(cols[:], w["cols"]).then_inc(vec_in, 16)
            sp.dma_start(rows[:].rearrange("p a c -> p (a c)"), w["row_vectors"].to_broadcast([P, 4 * C])).then_inc(vec_in, 16)
            sp.wait_ge(vec_in, 32)

        @block.gpsimd
        def _(pool):
            steps = Steps(pool, made)
            ident, i2 = const["ident"], const["ident2"]
            for tile, value in ((ones, 1.0), (ident, 0.0), (const["minus_ident"], 0.0), (i2, 0.0), (const["zeros"], 0.0), (const["mean"], 1.0 / HALF),
                                (const["ab_init"], 0.0)):
                steps.did(pool.memset(tile[:], value))
            for j, value in enumerate(SCALARS):
                steps.did(pool.memset(const["scalars"][:, j:j + 1], value))
            steps.settle()
            for tile, value in ((ident, 1.0), (const["minus_ident"], -1.0)):
                steps.did(pool.affine_select(out=tile[:], in_=tile[:], compare_op=ALU.not_equal, fill=value, base=0,
                                             pattern=[[-1, P]], channel_multiplier=1))
            for lo in (0, HALF):
                steps.settle()
                part = slice(lo, lo + HALF)
                steps.did(pool.affine_select(out=i2[part], in_=i2[part], compare_op=ALU.not_equal, fill=1.0, base=0,
                                             pattern=[[-1, HALF]], channel_multiplier=1))
            steps.settle()
            steps.did(pool.memset(const["ab_init"][LO], 1.0))
            steps.settle()

        @block.scalar
        def _(act):
            act.wait_ge(w_in, 16)
            act.activation(size[:], wt[:], ACT.Abs, accum_out=small[:, 0:1]).then_inc(row_sums, 1)

        @block.tensor
        def _(pe):
            pe.wait_ge(made, 1)
            pe.wait_ge(row_sums, 1)
            pe.matmul(ps[:], ones[:], small[:, 0:1], start=True, stop=True).then_inc(total, 1)

        @block.vector
        def _(dve):
            steps = Steps(dve, own)
            dve.wait_ge(total, 1)
            steps.did(dve.tensor_scalar(small[:, 1:2], ps[:], 1.0 / (C * C), 1e-5, ALU.mult, ALU.max))
            steps.settle()
            steps.did(dve.tensor_scalar(small[:, 2:3], small[:, 1:2], 0.5, None, ALU.mult))
            steps.did(dve.tensor_scalar(small[:, 3:4], small[:, 1:2], -0.5, None, ALU.mult))
            steps.settle()
            steps.did(dve.tensor_scalar(size[:], wt[:], small[:, 2:3], small[:, 1:2], ALU.is_gt, ALU.mult))
            steps.did(dve.tensor_scalar(const["ternary"][:], wt[:], small[:, 3:4], small[:, 1:2], ALU.is_lt, ALU.mult))
            steps.settle()
            steps.did(dve.tensor_tensor(const["ternary"][:], size[:], const["ternary"][:], ALU.subtract))
            steps.settle()


def remember(nc, const, rows, w, mem, x2, hidT, out):
    with ExitStack() as ctx:
        def sb(name, shape, dt=F32):
            return ctx.enter_context(nc.sbuf_tensor("p4_" + name, shape, dt))

        def sem(name):
            return ctx.enter_context(nc.semaphore("p4_" + name))

        def two(name, shape):
            return [sb(f"{name}{s}", shape) for s in range(2)]

        kv, vT, kce, small = two("kv", [P, B, MC]), two("vT", [P, B, HALF]), two("kce", [P, B, P]), two("small", [P, B, 6])
        aqb, G, C_, ab = two("aqb", [P, B, MC]), two("G", [P, B, MC]), two("C", [P, B, MC]), two("ab", [P, B, MC])
        xr, hT = two("x", [P, B, C]), two("hT", [P, CH, B, P])
        ws1, ws2 = two("ws1", [P, B, P]), two("ws2", [P, B, P])
        aF, g1, g2 = two("aF", [P, B, MC]), two("g1", [P, B, 2, HALF]), two("g2", [P, B, 2, HALF])
        w_gate, w_o, w_t = sb("w_gate", [P, CH, C]), sb("w_o", [HALF, C]), const["ternary"]
        sgF, sgT, aT, ds, u = sb("sgF", [P, B, MC]), sb("sgT", [P, B, HALF]), sb("aT", [P, B, HALF]), sb("ds", [P, B, HALF]), sb("u", [P, B, HALF])
        w2 = sb("w2", [P, B, HALF])
        ace, mixer = sb("ace", [P, B, 2, HALF]), sb("mixer", [P, B, 2, HALF])
        eF, eT, dz = sb("eF", [P, B, MC]), sb("eT", [P, B, HALF]), sb("dz", [P, B, HALF])
        sq, sq_act = sb("sq", [P, B, HALF]), sb("sq_act", [P, 2, B, HALF])
        norms = sb("norms", [P, 8, B])
        sg2, h, hab, G2, rF = sb("sg2", [P, B, MC]), sb("h", [P, B, MC]), sb("hab", [P, B, MC]), sb("G2", [P, B, MC]), sb("rF", [HALF, B, MC])
        gate, gated, z, zT = sb("gate", [P, B, C]), sb("gated", [P, B, C]), sb("z", [P, B, C]), sb("zT", [P, CH, B * P])
        factor = sb("factor", [P, B])
        junk = sb("junk", [P, B, C])
        ms = sb("ms", [P, 4, B])
        stats, mv, rstd, tmp = sb("stats", [P, B, 6]), sb("mv", [P, B, 2]), sb("rstd", [P, B]), sb("tmp", [P, B])
        bank = [ctx.enter_context(nc.psum_tensor(f"p4_bank{i}", [P, CHUNK], F32)) for i in range(4)]
        ps_o = ctx.enter_context(nc.psum_tensor("p4_o", [P, 2, 2, C], F32))
        ps_g = ctx.enter_context(nc.psum_tensor("p4_g", [P, 2, CHUNK], F32))

        def cols(b, n):
            return slice(b * n, (b + 1) * n)

        w_in, set0 = sem("weights_loaded"), sem("states_zeroed")
        chain_in, out_in = [sem("chain_terms0"), sem("chain_terms1")], [sem("output_terms0"), sem("output_terms1")]
        z_ready, sg_ready, aF_ready, aT_ready = map(sem, ("z1_in_psum", "sigmoids_and_w2", "aF", "aT"))
        p_ready, e_ready, da_ready, pool_ready = map(sem, ("predictions_in_psum", "eF_and_eT", "da_in_psum", "mixer_slope_ace"))
        squares_a, squares_e, norm_ready, pow_ready, g_ready, st_ready, ws_ready = map(sem, (
            "a_norms", "e_norms", "gradient_norms", "inverse_norms", "gradients", "states_in_psum", "states"))
        z2_ready, sg2_ready, h_ready, ah_ready, G2_ready, hab_ready, r_ready, rF_ready = map(sem, (
            "z2_in_psum", "sigmoid_2", "h", "ah_in_psum", "G2", "h_scaled", "r_in_psum", "rF"))
        gate_ready, o_ready, ms_ready, rms_ready, gate_taken, gated_ready, x3_ready = map(sem, (
            "gate_in_psum", "out_in_psum", "mean_squares", "inverse_rms", "gate", "gate_normed", "x3"))
        y_ready, var_ready, rstd_ready, zn_ready, zT_turned, zT_ready, f_ready, x4_ready, x4_out = map(sem, (
            "y", "variance", "rstd", "z", "zT_in_psum", "zT", "ffn_in_psum", "x4", "x4_stored"))
        da_taken, passed = sem("da_taken"), sem("passed")
        NORM_STEPS, WEIGHTS = B + 4, 16 * 4
        own_n, own_s, own_p, own_a = map(sem, ("norm_steps", "stats_steps", "pool_steps", "pool_slope_steps"))
        passed_dve = sem("passed_dve")
        tok = lambda a: a.rearrange("(b c p) n -> c p b n", b=B, p=P)
        x2_c, out_c, hT_c = tok(x2), tok(out), hidT.rearrange("b p g (c t) -> c p g b t", t=MC)

        def terms(name, c):
            m = mem[name]
            if len(m.shape) == 3:
                m = m.rearrange("p (b c) n -> p c b n", b=B)
            else:
                m = m.rearrange("p (b c n) -> p c b n", b=B, c=NM)
            return m[:, bass.ds(c, 1)].rearrange("p o b n -> p (o b) n")

        block = ctx.enter_context(nc.Block())

        @block.sync
        def _(sp):
            def load_chain(c, s):
                if not isinstance(c, int):
                    sp.wait_ge(ws_ready, 2 * (c - 1))
                for dst, name in ((kv[s][:], "kv"), (vT[s][:], "vT"), (kce[s][:], "kce"), (small[s][:], "small")):
                    sp.dma_start(dst, terms(name, c)).then_inc(chain_in[s], 16)

            def load_out(c, s):
                if not (isinstance(c, int) and c < 2):
                    sp.wait_ge(x4_out, 16 * (c - 1))
                for dst, name in ((aqb, "aqb"), (G, "G"), (C_, "C"), (ab, "ab")):
                    sp.dma_start(dst[s][:], terms(name, c)).then_inc(out_in[s], 16)
                sp.dma_start(xr[s][:], x2_c[c]).then_inc(out_in[s], 16)
                for g in range(CH):
                    sp.dma_start(hT[s][:, g], hT_c[c][:, g]).then_inc(out_in[s], 16)

            def store(c, s):
                sp.wait_ge(x4_ready, 2 * c + 2)
                sp.dma_start(out_c[c], xr[s][:]).then_inc(x4_out, 16)

            for tile, name in ((ws1, "m1T"), (ws2, "m2T")):
                sp.dma_start(tile[0][LO].rearrange("p b (j n) -> p (b j) n", j=2),
                             w[name].unsqueeze(1).to_broadcast([HALF, 2 * B, HALF])).then_inc(w_in, 16)
            load_chain(0, 0)
            sp.dma_start(w_gate[:], w["w_gate"].rearrange("(g p) n -> p g n", p=P)).then_inc(w_in, 16)
            sp.dma_start(w_o[:], w["w_o"]).then_inc(w_in, 16)
            load_chain(1, 1)
            load_out(0, 0)
            with sp.Fori(0, NM // 2 - 1) as r:
                for s in (1, 0):
                    c = 2 * r + 2 - s
                    load_chain(c + 1, 1 - s)
                    load_out(c, s)
                    store(c - 1, 1 - s)
            load_out(NM - 1, 1)
            store(NM - 2, 0)
            store(NM - 1, 1)
            sp.wait_ge(x4_out, 16 * NM)

        @block.tensor
        def _(pe):
            ident = const["ident"]

            def each(fn, done):
                for b in range(B):
                    ins = fn(b)
                ins.then_inc(done, 1)

            def c1(c, s):
                pe.wait_ge(chain_in[s], 16 * 4 * ((c - s) // 2 + 1))
                pe.wait_ge(ws_ready, 2 * c)
                pe.sem_inc(passed, 1)
                each(lambda b: pe.matmul(bank[0][LO, cols(b, MC)], ws1[s][LO, b, 0:HALF], kv[s][LO, b], start=True, stop=True), z_ready)
                pe.wait_ge(norm_ready, c)
                each(lambda b: pe.matmul(bank[1][:, cols(b, HALF)], kv[s][LO, b], ws1[s][LO, b, 0:HALF], start=True, stop=True), z_ready)
                each(lambda b: pe.transpose(bank[2][:, cols(b, HALF)], ws2[s][LO, b], ident[LO, 0:HALF]), z_ready)

            def c2(c, s):
                pe.wait_ge(aF_ready, c + 1)
                pe.sem_inc(passed, 1)
                each(lambda b: pe.matmul(bank[0][HI, cols(b, MC)], ws2[s][LO, b, 0:HALF], aF[s][LO, b], start=True, stop=True), p_ready)
                pe.wait_ge(aT_ready, c + 1)
                each(lambda b: pe.matmul(bank[1][:, cols(b, HALF)], aF[s][LO, b], ws2[s][LO, b, 0:HALF], start=True, stop=True), p_ready)

            def c3(c, s):
                pe.wait_ge(sg_ready, 3 * c + 3)
                pe.wait_ge(e_ready, 2 * c + 2)
                each(lambda b: pe.matmul(bank[1][:, cols(b, HALF)], eF[HI, b], w2[HI, b], start=True, stop=True), da_ready)

            def c4(c, s):
                pe.wait_ge(pool_ready, 3 * c + 3)
                pe.wait_ge(g_ready, 2 * c + 2)
                for j, (lhs, grad, state) in enumerate(((kce[s], g1[s], ws1[s]), (ace, g2[s], ws2[s]))):
                    for b in range(B):
                        o_b = bank[2 * j][:, cols(b, P)]
                        lhs_b = lhs[:, b] if j == 0 else lhs[:, b].rearrange("p a n -> p (a n)")
                        pe.matmul(o_b, lhs_b, grad[:, b].rearrange("p a n -> p (a n)"), start=True, stop=False)
                        ins = pe.matmul(o_b, mixer[:, b].rearrange("p a n -> p (a n)"), state[:, b], start=False, stop=True)
                    ins.then_inc(st_ready, 1)

            def o1(c, s):
                pe.wait_ge(out_in[s], 16 * 7 * ((c - s) // 2 + 1))
                pe.wait_ge(rF_ready, c)
                for b in range(B):
                    o_b = bank[3][:, cols(b, MC)]
                    pe.matmul(o_b, g1[s][:, b].rearrange("p a n -> p (a n)"), G[s][:, b], start=True, stop=False)
                    ins = pe.matmul(o_b, ws1[s][:, b], aqb[s][:, b], start=False, stop=True)
                ins.then_inc(z2_ready, 1)

            def o2(c, s):
                pe.wait_ge(h_ready, c + 1)
                each(lambda b: pe.matmul(bank[3][:, cols(b, MC)], aF[s][LO, b], h[LO, b], start=True, stop=True), ah_ready)

            def gates(c, s):
                pe.wait_ge(zT_ready, c)
                for b in range(B):
                    for g in range(CH):
                        ins = pe.matmul(ps_g[:, b // 2, cols(b % 2, C)], hT[s][:, g, b], w_gate[:, g], start=g == 0, stop=g == CH - 1)
                ins.then_inc(gate_ready, 1)

            def o3(c, s):
                pe.wait_ge(G2_ready, c + 1)
                pe.wait_ge(hab_ready, c + 1)
                for b in range(B):
                    o_b = bank[3][LO, cols(b, MC)]
                    pe.matmul(o_b, g2[s][:, b, 0], G2[:, b], start=True, stop=False)
                    ins = pe.matmul(o_b, ws2[s][:, b, 0:HALF], hab[:, b], start=False, stop=True)
                ins.then_inc(r_ready, 1)

            def o4(c, s):
                pe.wait_ge(rF_ready, c + 1)
                pe.wait_ge(x4_ready, 2 * c)
                each(lambda b: pe.matmul(ps_o[:, b // 2, b % 2], rF[:, b], w_o[:], start=True, stop=True), o_ready)

            def turn(c, s):
                pe.wait_ge(zn_ready, c + 1)
                pe.wait_ge(gate_taken, c + 1)
                for g in range(CH):
                    for b in range(B):
                        ins = pe.transpose(ps_g[:, g, cols(b, P)], z[:, b, g * P:(g + 1) * P], ident[:])
                ins.then_inc(zT_turned, 1)

            def ffn(c, s):
                pe.wait_ge(zT_ready, c + 1)
                for b in range(B):
                    for g in range(CH):
                        ins = pe.matmul(ps_o[:, b // 2, b % 2], zT[:, g, cols(b, P)], w_t[:, g], start=g == 0, stop=g == CH - 1)
                    if b % 2:
                        ins.then_inc(f_ready, 1)

            def step(c, s, chain=True, outputs=True):
                t = 1 - s
                if chain: c1(c, s)
                if outputs: o1(c - 1, t)
                if chain: c2(c, s)
                if outputs: o2(c - 1, t)
                if chain: c3(c, s)
                if outputs:
                    gates(c - 1, t)
                    o3(c - 1, t)
                    o4(c - 1, t)
                if chain: c4(c, s)
                if outputs:
                    turn(c - 1, t)
                    ffn(c - 1, t)

            pe.wait_ge(w_in, WEIGHTS)
            pe.wait_ge(set0, 2)
            step(0, 0, outputs=False)
            with pe.Fori(0, NM // 2 - 1) as r:
                for s in (1, 0):
                    step(2 * r + 2 - s, s)
            step(NM - 1, 1)
            step(NM, 0, chain=False)

        @block.scalar
        def _(act):
            def c1(c, s):
                act.wait_ge(z_ready, 3 * c + 1)
                act.activation(sgF[LO], bank[0][LO].rearrange("p (b n) -> p b n", b=B), ACT.Sigmoid).then_inc(sg_ready, 1)
                act.wait_ge(z_ready, 3 * c + 2)
                act.activation(sgT[:], bank[1][:, 0:B * HALF].rearrange("p (b n) -> p b n", b=B), ACT.Sigmoid).then_inc(sg_ready, 1)
                act.wait_ge(z_ready, 3 * c + 3)
                act.activation(w2[HI], bank[2][HI, 0:B * HALF].rearrange("p (b n) -> p b n", b=B), ACT.Copy).then_inc(sg_ready, 1)

            def squares(src, j, ready, count, done):
                act.wait_ge(ready, count)
                for b in range(B):
                    act.activation(sq_act[:, j, b], src[:, b], ACT.Square, accum_out=norms[:, j, b:b + 1]).then_inc(done, 1)

            def c4(c, s):
                for j, state in enumerate((ws1, ws2)):
                    act.wait_ge(st_ready, 2 * c + j + 1)
                    act.activation(state[1 - s][:], bank[2 * j].rearrange("p (b n) -> p b n", b=B), ACT.Copy).then_inc(ws_ready, 1)

            def sigmoid2(c):
                act.wait_ge(z2_ready, c + 1)
                act.activation(sg2[:], bank[3].rearrange("p (b n) -> p b n", b=B), ACT.Sigmoid).then_inc(sg2_ready, 1)

            def r_out(c):
                act.wait_ge(r_ready, c + 1)
                act.activation(rF[:], bank[3][LO].rearrange("p (b n) -> p b n", b=B), ACT.Copy).then_inc(rF_ready, 1)

            def mean_squares(c):
                act.wait_ge(o_ready, c + 1)
                act.wait_ge(ms_ready, B * c)
                for b in range(B):
                    act.activation(junk[:, b], ps_o[:, b // 2, b % 2], ACT.Square, scale=C ** -0.5,
                                   accum_out=ms[:, 0, b:b + 1]).then_inc(ms_ready, 1)

            def copy_zT(c):
                act.wait_ge(zT_turned, c + 1)
                act.activation(zT[:], ps_g[:], ACT.Copy).then_inc(zT_ready, 1)

            def step(c, s, chain=True, outputs=True):
                if chain: c1(c, s)
                if outputs: sigmoid2(c - 1)
                if chain:
                    squares(aT, 0, aT_ready, c + 1, squares_a)
                    squares(eT, 1, e_ready, 2 * c + 2, squares_e)
                if outputs:
                    r_out(c - 1)
                    mean_squares(c - 1)
                if chain: c4(c, s)
                if outputs: copy_zT(c - 1)

            step(0, 0, outputs=False)
            with act.Fori(0, NM // 2 - 1) as r:
                for s in (1, 0):
                    step(2 * r + 2 - s, s)
            step(NM - 1, 1)
            step(NM, 0, chain=False)
            act.wait_ge(ws_ready, 2 * NM)

        @block.gpsimd
        def _(pool):
            def wide(ap):
                return ap.to_broadcast([P, B, HALF])

            def c1(c, s):
                pool.wait_ge(chain_in[s], 16 * 4 * ((c - s) // 2 + 1))
                pool.wait_ge(ws_ready, 2 * c)
                ident2 = const["ident2"][:].unsqueeze(1).to_broadcast([P, B, HALF])
                for j in range(2):
                    ins = pool.tensor_tensor(mixer[:, :, j], ident2, wide(small[s][:, :, 2 + j:3 + j]), ALU.mult)
                ins.then_inc(pool_ready, 1)
                pool.wait_ge(sg_ready, 3 * c + 2)
                pool.tensor_tensor(u[:], sgT[:], scalar(const, S_ONE, u.shape), ALU.subtract).then_inc(own_a, 1)
                pool.wait_ge(own_a, 2 * c + 1)
                pool.wait_ge(aT_ready, c + 1)
                pool.tensor_tensor(u[:], u[:], aT[:], ALU.mult).then_inc(own_a, 1)
                pool.wait_ge(own_a, 2 * c + 2)
                pool.wait_ge(da_taken, c)
                pool.tensor_tensor(ds[:], sgT[:], u[:], ALU.subtract).then_inc(pool_ready, 1)
                for j in range(2):
                    ins = pool.tensor_tensor(ace[:, :, j], aT[:], wide(small[s][:, :, j:j + 1]), ALU.mult)
                ins.then_inc(pool_ready, 1)

            def power(src, dst, done):
                pool.tensor_tensor(dst, src, scalar(const, S_MINUS_HALF, [P, B]), ALU.pow).then_inc(done, 1)

            def scale_h(c, s):
                pool.wait_ge(h_ready, c + 1)
                pool.wait_ge(r_ready, c)
                pool.tensor_tensor(hab[:], h[:], ab[s][:], ALU.mult).then_inc(hab_ready, 1)

            def c4(c):
                pool.wait_ge(norm_ready, c + 1)
                power(norms[:, 6], norms[:, 7], pow_ready)

            def inverse_rms(c):
                pool.wait_ge(ms_ready, B * (c + 1))
                pool.tensor_tensor(ms[:, 1], ms[:, 0], scalar(const, S_RMS_EPS, [P, B]), ALU.add).then_inc(own_p, 1)
                pool.wait_ge(own_p, 2 * c + 1)
                power(ms[:, 1], ms[:, 2], rms_ready)

            def norm_gate(c):
                pool.wait_ge(gate_taken, c + 1)
                pool.wait_ge(y_ready, c)
                pool.tensor_tensor(gated[:], gate[:], rows[:, ROW_NORMG:ROW_NORMG + 1].to_broadcast([P, B, C]), ALU.mult).then_inc(gated_ready, 1)

            def deviation(c):
                pool.wait_ge(var_ready, c + 1)
                steps = Steps(pool, own_p)
                steps.at(2 * c + 1)
                inverse_deviation(pool, steps, mv[:, :, 1], const, tmp[:], rstd[:], rstd_ready)

            def step(c, s, chain=True, outputs=True):
                t = 1 - s
                if chain: c1(c, s)
                if outputs: scale_h(c - 1, t)
                if outputs: norm_gate(c - 1)
                if chain: c4(c)
                if outputs:
                    inverse_rms(c - 1)
                    deviation(c - 1)

            step(0, 0, outputs=False)
            with pool.Fori(0, NM // 2 - 1) as r:
                for s in (1, 0):
                    step(2 * r + 2 - s, s)
            step(NM - 1, 1)
            step(NM, 0, chain=False)

        @block.vector
        def _(dve):
            dve.memset(ws1[0][HI], 0.0).then_inc(set0, 1)
            dve.memset(ws2[0][HI], 0.0).then_inc(set0, 1)
            norm_steps, stat_steps = Steps(dve, own_n), Steps(dve, own_s)

            def split(ap, n=B):
                return ap.rearrange("p (b n) -> p b n", b=n)

            def c1(c, s):
                dve.wait_ge(sg_ready, 3 * c + 1)
                dve.tensor_tensor(aF[s][LO], split(bank[0][LO]), sgF[LO], ALU.mult).then_inc(aF_ready, 1)
                dve.wait_ge(sg_ready, 3 * c + 2)
                dve.wait_ge(pool_ready, 3 * c)
                dve.wait_ge(squares_a, B * c)
                dve.tensor_tensor(aT[:], split(bank[1][:, 0:B * HALF]), sgT[:], ALU.mult).then_inc(aT_ready, 1)

            def c2(c, s):
                dve.wait_ge(p_ready, 2 * c + 1)
                dve.tensor_tensor(eF[HI], split(bank[0][HI]), kv[s][HI], ALU.subtract).then_inc(e_ready, 1)
                dve.wait_ge(p_ready, 2 * c + 2)
                dve.wait_ge(squares_e, B * c)
                dve.tensor_tensor(eT[:], split(bank[1][:, 0:B * HALF]), vT[s][:], ALU.subtract).then_inc(e_ready, 1)

            def c3(c, s):
                dve.wait_ge(da_ready, c + 1)
                dve.wait_ge(pool_ready, 3 * c + 2)
                norm_steps.at(NORM_STEPS * c)
                dve.tensor_tensor(dz[:], split(bank[1][:, 0:B * HALF]), ds[:], ALU.mult).then_inc(da_taken, 1)
                dve.wait_ge(da_taken, c + 1)
                for b in range(B):
                    norm_steps.did(dve.tensor_tensor_reduce(sq[:, b], dz[:, b], dz[:, b], 1.0, 0.0, ALU.mult, ALU.add, norms[:, 2, b:b + 1]))
                dve.wait_ge(squares_a, B * (c + 1))
                dve.wait_ge(squares_e, B * (c + 1))
                norm_steps.did(dve.tensor_tensor(norms[:, 3], norms[:, 0], norms[:, 1], ALU.mult))
                norm_steps.settle()
                norm_steps.did(dve.tensor_tensor(norms[:, 4], norms[:, 2], small[s][:, :, 5], ALU.mult))
                norm_steps.settle()
                norm_steps.did(dve.tensor_tensor(norms[:, 5], norms[:, 3], norms[:, 4], ALU.add))
                norm_steps.settle()
                dve.tensor_scalar(norms[:, 6], norms[:, 5], 0.04, RMS_EPS ** 2, ALU.mult, ALU.max).then_inc(norm_ready, 1)
                dve.wait_ge(pow_ready, c + 1)
                norm_steps.did(dve.scalar_tensor_tensor(out=factor[:], in0=norms[:, 7], scalar=1.0, in1=small[s][:, :, 4], op0=ALU.min, op1=ALU.mult))
                norm_steps.settle()
                for src, dst in ((dz, g1), (eT, g2)):
                    dve.tensor_tensor(dst[s][:], src[:].unsqueeze(2).to_broadcast([P, B, 2, HALF]),
                                      factor[:].unsqueeze(2).unsqueeze(3).to_broadcast([P, B, 2, HALF]), ALU.mult).then_inc(g_ready, 1)

            def o1(c, s):
                dve.wait_ge(sg2_ready, c + 1)
                dve.wait_ge(hab_ready, c)
                dve.tensor_tensor(h[:], split(bank[3][:]), sg2[:], ALU.mult).then_inc(h_ready, 1)

            def o2(c, s):
                dve.wait_ge(ah_ready, c + 1)
                dve.tensor_tensor(G2[:], split(bank[3][:]), C_[s][:], ALU.mult).then_inc(G2_ready, 1)

            def take_gate(c):
                dve.wait_ge(gate_ready, c + 1)
                dve.wait_ge(gated_ready, c)
                dve.tensor_tensor(gate[:], ps_g.rearrange("p a (k n) -> p (a k) n", n=C), rows[:, ROW_GB:ROW_GB + 1].to_broadcast([P, B, C]),
                                  ALU.add).then_inc(gate_taken, 1)

            def combine(c, s):
                dve.wait_ge(rms_ready, c + 1)
                dve.wait_ge(gated_ready, c + 1)
                stat_steps.at((2 * B) * c)
                for b in range(B):
                    stat_steps.did(dve.scalar_tensor_tensor(out=gated[:, b], in0=ps_o[:, b // 2, b % 2], scalar=ms[:, 2, b:b + 1], in1=gated[:, b],
                                                            op0=ALU.mult, op1=ALU.mult))
                stat_steps.settle()
                dve.tensor_tensor(xr[s][:], xr[s][:], gated[:], ALU.add).then_inc(y_ready, 1)
                dve.wait_ge(y_ready, c + 1)
                moments(dve, stat_steps, xr[s], stats, mv, var_ready, passed_dve)

            def finish(c, s):
                dve.wait_ge(rstd_ready, c + 1)
                dve.wait_ge(zT_turned, c)
                normalise(dve, xr[s], mv, rstd, z, zn_ready)

            def add_ffn(c, s):
                for k in range(2):
                    dve.wait_ge(f_ready, 2 * c + k + 1)
                    x_k = xr[s][:, 2 * k:2 * k + 2]
                    dve.tensor_tensor(x_k, x_k, ps_o[:, k], ALU.add).then_inc(x4_ready, 1)

            def step(c, s, chain=True, outputs=True):
                t = 1 - s
                if chain: c1(c, s)
                if outputs: o1(c - 1, t)
                if chain: c2(c, s)
                if outputs:
                    o2(c - 1, t)
                    take_gate(c - 1)
                if chain: c3(c, s)
                if outputs:
                    combine(c - 1, t)
                    finish(c - 1, t)
                    add_ffn(c - 1, t)

            step(0, 0, outputs=False)
            with dve.Fori(0, NM // 2 - 1) as r:
                for s in (1, 0):
                    step(2 * r + 2 - s, s)
            step(NM - 1, 1)
            step(NM, 0, chain=False)


_INS = ["x", "w_qkv", "cols", "row_vectors", "w_ffn", "w_out", "w_p", "w_gate", "w_o", "m1T", "m2T"]


def build(nc, t, out):
    with ExitStack() as ctx:
        def sb(name, shape, dt=F32):
            return ctx.enter_context(nc.sbuf_tensor(name, shape, dt))

        def dram(name, shape, dt=F32):
            return nc.dram_tensor(name, shape, dt).ap()

        cols, rows = sb("cols", [P, NCOLS]), sb("rows", [P, 4, C])
        const = {"ident": sb("ident", [P, P]), "minus_ident": sb("minus_ident", [P, P]), "ident2": sb("ident2", [P, HALF]),
                 "zeros": sb("zeros", [P, MC]), "mean": sb("mean", [P, P]), "scalars": sb("scalars", [P, len(SCALARS)]),
                 "ab_init": sb("ab_init", [P, 1]), "ternary": sb("ternary", [P, CH, C])}
        qk_parts = dram("qk_parts", (2, B * C, PARTS, T), BF16)
        xres, x2 = dram("xres", (TOK, C)), dram("x2", (TOK, C))
        oT, inverse = dram("oT", (NG * P, T)), dram("inverse_sums", (B * H, T))
        hidT = dram("hidT", (B, P, CH, T))

        constants(nc, const, cols, rows, t)
        with ExitStack() as attention:
            v_all = attention.enter_context(nc.sbuf_tensor("v_all", [P, NG, KT, CG], F32))
            project(nc, t["x"], t["w_qkv"], cols, rows, const, qk_parts, v_all, xres)
            attend(nc, qk_parts, v_all, oT, inverse)
        mem = {"kv": dram("m_kv", (P, TOK)), "aqb": dram("m_aqb", (P, TOK)), "C": dram("m_C", (P, TOK)), "G": dram("m_G", (P, TOK)),
               "ab": dram("m_ab", (P, TOK)), "kce": dram("m_kce", (P, NT, P)), "vT": dram("m_vT", (P, NT, HALF)), "small": dram("m_small", (P, NT, 6))}
        mix(nc, const, cols, t, oT, inverse, xres, x2, hidT, mem)
        remember(nc, const, rows, t, mem, x2, hidT, out.rearrange("b t c -> (b t) c"))


_OUTS = [((B, T, C), "float32")]


def lay_out(inp):
    attn = lambda n: inp["L0_attn_a_" + n]
    memo = lambda n: inp["L0_attn_b_" + n]
    a = {"x": attn("x").reshape(TOK, C), "w_qkv": attn("w_qkv"), "w_out": attn("w_out"),
         "w_ffn": inp["L0_ffn_weight"].T, "w_gate": memo("gW").T, "w_o": memo("Wo").T, "m1T": memo("mW1").T, "m2T": memo("mW2").T,
         "w_p": np.concatenate([memo(n) for n in ("Wk", "eW", "Wq", "tW", "Wv", "aW")]).T}
    cols = np.zeros((P, NCOLS), np.float32)
    for v, at in ((attn("ln_gamma"), COL_GAMMA), (attn("ln_beta"), COL_BETA), (attn("b_qkv")[:2 * C], COL_BQK)):
        cols[:, at:at + v.size // P] = v.reshape(-1, P).T
    for at, n in ((COL_K, "ck"), (COL_Q, "cq"), (COL_V, "cv")):
        cols[:HALF, at:at + 4] = memo(n + "w")
        cols[:HALF, at + 4] = memo(n + "b")
    for j, n in enumerate(("eb", "tb", "ab")):
        cols[HALF:, COL_GATE_B + j] = memo(n)
    a["cols"] = cols
    a["row_vectors"] = np.concatenate([attn("b_qkv")[2 * C:], attn("b_out"), memo("norm_g"), memo("gb")]).reshape(1, 4 * C)
    return {k: np.ascontiguousarray(v) for k, v in a.items()}


def kernel(**inputs):
    import numpy as _np
    import concourse.bacc as _bacc
    from concourse import mybir as _mybir
    from concourse.bass_utils import run_bass_kernel_spmd as _run

    nc = _bacc.Bacc("TRN2", target_bir_lowering=False, num_devices=1)
    laid = lay_out({name: _np.asarray(a) for name, a in inputs.items()})
    arrays = {f"in_{name}_dram": laid[name] for name in _INS}
    t = {name: nc.dram_tensor(f"in_{name}_dram", laid[name].shape, _mybir.dt.from_np(laid[name].dtype), kind="ExternalInput").ap()
         for name in _INS}
    shape, dtype = _OUTS[0]
    out = nc.dram_tensor("out_0_dram", shape, _mybir.dt.from_np(_np.dtype(dtype)), kind="ExternalOutput").ap()
    build(nc, t, out)
    r = _run(nc, [arrays], core_ids=[0])
    return r.results[0]["out_0_dram"]
```

```python
from contextlib import ExitStack

import numpy as np
import concourse.bass as bass
from concourse import mybir

ALU = mybir.AluOpType
ACT = mybir.ActivationFunctionType
AX = mybir.AxisListType
F32 = mybir.dt.float32
BF16 = mybir.dt.bfloat16

P = 128
B, T, C = 4, 1024, 256
TOK = B * T
H, HD = 16, 16
CH = C // P
CHUNK = 512
NCH = TOK // CHUNK
TPC = CHUNK // P
NT = TOK // P
LN_EPS = 1e-5
RMS_EPS = 1e-6


class Steps:

    def __init__(self, eng, sem):
        self.eng, self.sem, self.base, self.k = eng, sem, 0, 0

    def at(self, base):
        self.base, self.k = base, 0

    def did(self, ins):
        self.k += 1
        ins.then_inc(self.sem, 1)

    def settle(self):
        self.eng.wait_ge(self.sem, self.base + self.k)


COL_GAMMA, COL_BETA, COL_BQK = 0, 2, 4
COL_KV, COL_Q = 8, 13
COL_GATE_B, COL_THETA_B = 18, 19
NCOLS = 20
ROW_BV, ROW_BOUT, ROW_NORMG, ROW_GB = range(4)

def retire(nc, sems):
    nc.clear_and_free_semaphores(sems)
    nc.all_engine_barrier()


def moments(dve, steps, src, stats, mv, ready, passed):
    n = src.shape[1]
    for i in range(n):
        steps.did(dve.bn_stats(stats[:, i, :], src[:, i, :]))
    steps.settle()
    dve.sem_inc(passed, 1)
    for i in range(n):
        ins = dve.bn_aggr(mv[:, i, :], stats[:, i, :])
    ins.then_inc(ready, 1)


def normalise(dve, src, mv, rstd, dst, ready):
    n = src.shape[1]
    for i in range(n):
        ins = dve.tensor_scalar(dst[:, i, :], src[:, i, :], mv[:, i, 0:1], rstd[:, i:i + 1], ALU.subtract, ALU.mult)
    ins.then_inc(ready, 1)


SCALARS = (-0.5, LN_EPS, RMS_EPS, 1.0)
S_MINUS_HALF, S_LN_EPS, S_RMS_EPS, S_ONE = range(4)


def scalar(const, which, shape):
    col = const["scalars"][:, which:which + 1]
    for _ in shape[2:]:
        col = col.unsqueeze(len(col.shape))
    return col.to_broadcast(shape)


def inverse_deviation(pool, steps, var, const, tmp, rstd, ready):
    steps.did(pool.tensor_tensor(tmp, var, scalar(const, S_LN_EPS, tmp.shape), ALU.add))
    steps.settle()
    pool.tensor_tensor(rstd, tmp, scalar(const, S_MINUS_HALF, rstd.shape), ALU.pow).then_inc(ready, 1)


def project(nc, x, w_qkv, cols, rows, const, qk_parts, v_all, xres):
    with ExitStack() as ctx:
        def sb(name, shape, dt=F32):
            return ctx.enter_context(nc.sbuf_tensor(name, shape, dt))

        sems = []
        ctx.callback(retire, nc, sems)

        def sem(name):
            sems.append(nc.alloc_semaphore("p1_" + name))
            return sems[-1]

        wq = sb("wq", [P, CH, 3 * C])
        xin = sb("xin", [P, 2, TPC, C])
        y = sb("y", [P, 2, TPC, C])
        h = sb("h", [P, 2, TPC, C])
        hT = sb("hT", [P, 2, CH, CHUNK])
        res = sb("res", [P, 2, TPC, C])
        stats = sb("stats", [P, 2, TPC, 6])
        mv, rstd = sb("mv", [P, 2, TPC, 2]), sb("rstd", [P, 2, TPC])
        tmp = sb("var_eps", [P, TPC])
        rest = sb("rest", [P, 4, CHUNK])
        parts = sb("parts", [P, 4, 3, CHUNK], BF16)
        ps_t = ctx.enter_context(nc.psum_tensor("ps_t", [P, CH, CHUNK], F32))
        ps_qk = ctx.enter_context(nc.psum_tensor("ps_qk", [P, 4, CHUNK], F32))
        ps_v = ctx.enter_context(nc.psum_tensor("ps_v", [P, 2, 2, C], F32))

        w_in, x_in = sem("weights_loaded"), [sem("x_loaded_even"), sem("x_loaded_odd")]
        y_ready, h_ready, hT_ready = sem("y_ready"), sem("h_ready"), sem("hT_ready")
        y_added, hT_turned, v_ready = sem("y_added"), sem("hT_in_psum"), sem("v_in_psum")
        qk_ready, hi_ready, rest_ready = sem("qk_in_psum"), sem("hi_ready"), sem("rest_ready")
        mid_ready, lo_ready = sem("mid_ready"), sem("lo_ready")
        parts_out = [sem(f"parts_{j}_stored") for j in range(4)]
        var_x, var_y, rstd_x, rstd_y = sem("var_x_ready"), sem("var_y_ready"), sem("rstd_x_ready"), sem("rstd_y_ready")
        v_taken, own, pool_own = sem("v_taken"), sem("vector_steps"), sem("pool_steps")
        res_ready, passed = sem("res_ready"), sem("passed")
        res_out = [sem("res_stored_even"), sem("res_stored_odd")]
        xres_c = xres.rearrange("(n i p) c -> n p i c", i=TPC, p=P)
        x_c = x.rearrange("(n i p) c -> n p i c", i=TPC, p=P)
        ROUNDS = NCH // 2
        block = ctx.enter_context(nc.Block())

        @block.sync
        def _(sp):
            def store(r, s):
                sp.wait_ge(res_ready, 2 * r + s + 1)
                sp.dma_start(xres_c[2 * r + s], res[:, s]).then_inc(res_out[s], 16)
                for j in range(4):
                    sp.wait_ge(lo_ready, 4 * (2 * r + s) + j + 1)
                    dst = qk_parts[j // 2, bass.ds(C * r + P * (j % 2), P), :, s * CHUNK:(s + 1) * CHUNK]
                    sp.dma_start(dst, parts[:, j]).then_inc(parts_out[j], 16)

            for s in range(2):
                sp.dma_start(xin[:, s], x_c[s]).then_inc(x_in[s], 16)
            sp.dma_start(wq[:], w_qkv.rearrange("(g p) n -> p g n", p=P)).then_inc(w_in, 16)
            with sp.Fori(0, ROUNDS - 1) as r:
                for s in range(2):
                    store(r, s)
            for s in range(2):
                store(ROUNDS - 1, s)
            for stored in parts_out:
                sp.wait_ge(stored, 16 * NCH)
            for stored in res_out:
                sp.wait_ge(stored, 16 * ROUNDS)

        @block.vector
        def _(dve):
            steps = Steps(dve, own)

            def norm_x(r, s):
                dve.wait_ge(x_in[s], 16 * r + 16)
                moments(dve, steps, xin[:, s], stats[:, 0], mv[:, 0], var_x, passed)

            def norm_y(r, s):
                n = 2 * r + s
                dve.wait_ge(rstd_x, n + 1)
                dve.wait_ge(y_added, n)
                normalise(dve, xin[:, s], mv[:, 0], rstd[:, 0], y[:, s], y_ready)
                dve.wait_ge(y_ready, n + 1)
                moments(dve, steps, y[:, s], stats[:, 1], mv[:, 1], var_y, passed)

            def norm_h(r, s):
                n = 2 * r + s
                dve.wait_ge(rstd_y, n + 1)
                dve.wait_ge(hT_turned, n)
                normalise(dve, y[:, s], mv[:, 1], rstd[:, 1], h[:, s], h_ready)

            def left(r, s, j):
                n = 2 * r + s
                dve.wait_ge(hi_ready, 4 * n + j + 1)
                if j == 0:
                    dve.wait_ge(lo_ready, 4 * n)
                dve.scalar_tensor_tensor(out=rest[:, j], in0=ps_qk[:, j], scalar=cols[:, COL_BQK + j:COL_BQK + j + 1],
                                         in1=parts[:, j, 0], op0=ALU.add, op1=ALU.subtract).then_inc(rest_ready, 1)

            def values(r, s):
                n = 2 * r + s
                for i in range(2):
                    dve.wait_ge(v_ready, 2 * n + i + 3)
                    k = TPC * s + 2 * i
                    for t in range(2):
                        ins = dve.tensor_tensor(v_all[:, bass.ds(4 * r, 4), k + t], ps_v[:, i, t].rearrange("p (g c) -> p g c", g=4),
                                                rows[:, ROW_BV].rearrange("p (g c) -> p g c", g=4), ALU.add)
                    ins.then_inc(v_taken, 1)

            def step(r, s, after):
                steps.at(2 * TPC * (2 * r + s + 2))
                if after:
                    norm_x(r + 1, s)
                left(r, s, 0)
                if after:
                    norm_y(r + 1, s)
                for j in range(1, 4):
                    left(r, s, j)
                if after:
                    norm_h(r + 1, s)
                values(r, s)

            for s in range(2):
                steps.at(2 * TPC * s)
                norm_x(0, s)
                norm_y(0, s)
                norm_h(0, s)
            with dve.Fori(0, ROUNDS - 1) as r:
                for s in range(2):
                    step(r, s, True)
            for s in range(2):
                step(ROUNDS - 1, s, False)

        @block.gpsimd
        def _(pool):
            pool.sem_inc(y_added, 1)

            steps = Steps(pool, pool_own)

            def deviation(r, s, k, var_ready, ready):
                n = 2 * r + s
                pool.wait_ge(var_ready, n + 1)
                steps.at(2 * n + k)
                inverse_deviation(pool, steps, mv[:, k, :, 1], const, tmp[:], rstd[:, k], ready)

            def residual(r, s):
                n = 2 * r + s
                at = res[:, s]
                pool.wait_ge(y_ready, n + 1)
                pool.wait_ge(res_out[s], 16 * r)
                pool.tensor_tensor(at, xin[:, s], y[:, s], ALU.add).then_inc(y_added, 1)
                pool.wait_ge(y_added, n + 2)
                pool.tensor_tensor(at, at, rows[:, ROW_BOUT:ROW_BOUT + 1].to_broadcast([P, TPC, C]), ALU.add).then_inc(res_ready, 1)

            def low(r, s, j):
                n = 2 * r + s
                pool.wait_ge(mid_ready, 4 * n + j + 1)
                pool.tensor_tensor(parts[:, j, 2], rest[:, j], parts[:, j, 1], ALU.subtract).then_inc(lo_ready, 1)

            def step(r, s, after):
                if after:
                    deviation(r + 1, s, 0, var_x, rstd_x)
                low(r, s, 0)
                if after:
                    deviation(r + 1, s, 1, var_y, rstd_y)
                for j in range(1, 4):
                    low(r, s, j)
                if after:
                    residual(r + 1, s)

            for s in range(2):
                deviation(0, s, 0, var_x, rstd_x)
                deviation(0, s, 1, var_y, rstd_y)
                residual(0, s)
            with pool.Fori(0, ROUNDS - 1) as r:
                for s in range(2):
                    step(r, s, True)
            for s in range(2):
                step(ROUNDS - 1, s, False)

        @block.scalar
        def _(act):
            def load(r, s):
                act.wait_ge(y_added, 2 * r + s)
                act.dma_start(xin[:, s], x_c[2 * r + s]).then_inc(x_in[s], 16)

            def turned(r, s):
                n = 2 * r + s
                act.wait_ge(hT_turned, n + 2)
                act.wait_ge(v_ready, 2 * n)
                for c in range(CH):
                    ins = act.activation(hT[:, s, c], ps_t[:, c], ACT.Identity, bias=cols[:, COL_BETA + c:COL_BETA + c + 1],
                                         scale=cols[:, COL_GAMMA + c:COL_GAMMA + c + 1])
                ins.then_inc(hT_ready, 1)

            def splits(r, s):
                n = 2 * r + s
                for j in range(5):
                    if j < 4:
                        act.wait_ge(qk_ready, 4 * n + j + 1)
                        act.wait_ge(parts_out[j], 16 * n)
                        act.activation(parts[:, j, 0], ps_qk[:, j], ACT.Identity,
                                       bias=cols[:, COL_BQK + j:COL_BQK + j + 1]).then_inc(hi_ready, 1)
                    if j:
                        act.wait_ge(rest_ready, 4 * n + j)
                        act.activation(parts[:, j - 1, 1], rest[:, j - 1], ACT.Identity).then_inc(mid_ready, 1)

            turned(0, 0)
            with act.Fori(0, ROUNDS - 1) as r:
                for s in range(2):
                    load(r + 1, s)
                    turned(r + s, 1 - s)
                    splits(r, s)
            turned(ROUNDS - 1, 1)
            splits(ROUNDS - 1, 0)
            splits(ROUNDS - 1, 1)

        @block.tensor
        def _(pe):
            pe.sem_inc(hT_turned, 1)
            pe.sem_inc(v_ready, 2)

            def transposes(r, s):
                n = 2 * r + s
                pe.wait_ge(h_ready, n + 1)
                pe.wait_ge(hT_ready, n)
                for c in range(CH):
                    for i in range(TPC):
                        ins = pe.transpose(ps_t[:, c, i * P:(i + 1) * P], h[:, s, i, c * P:(c + 1) * P], const["ident"][:])
                ins.then_inc(hT_turned, 1)

            def products(r, s):
                n = 2 * r + s
                pe.wait_ge(hT_ready, n + 1)
                for j in range(4):
                    pe.wait_ge(rest_ready, 4 * n)
                    for c in range(CH):
                        ins = pe.matmul(ps_qk[:, j], wq[:, c, j * P:(j + 1) * P], hT[:, s, c], start=c == 0, stop=c == CH - 1)
                    ins.then_inc(qk_ready, 1)
                for i in range(TPC):
                    if i % 2 == 0:
                        pe.wait_ge(v_taken, 2 * n)
                    for c in range(CH):
                        ins = pe.matmul(ps_v[:, i // 2, i % 2], hT[:, s, c, i * P:(i + 1) * P], wq[:, c, 2 * C:],
                                        start=c == 0, stop=c == CH - 1)
                    if i % 2:
                        ins.then_inc(v_ready, 1)

            pe.wait_ge(w_in, 16)
            transposes(0, 0)
            with pe.Fori(0, ROUNDS - 1) as r:
                for s in range(2):
                    transposes(r + s, 1 - s)
                    products(r, s)
            transposes(ROUNDS - 1, 1)
            products(ROUNDS - 1, 0)
            products(ROUNDS - 1, 1)


GH = 4
NG = B * H // GH
CG = GH * HD
QC = T // CHUNK
KT = T // P
PARTS = 3
PAIRS = 6
Q_PART = (0, 0, 1, 1, 0, 2)
K_PART = (0, 1, 0, 1, 2, 0)
MROW = PAIRS * HD
ROWS = MROW + 2
SLOTS = 3
P_RING = 3
M_RING = 3
M_MMS = GH * (CHUNK // P) * (T // CHUNK)


def sums_of(oT, batches, per_head):
    rows = slice(batches.start * NG // B * P, batches.stop * NG // B * P)
    return oT[rows].rearrange("(h r) (j t) -> r h j t", r=2 * HD, j=per_head)[HD]


def inverses_of(inverse, batches, per_head):
    return inverse[batches.start * H:batches.stop * H].rearrange("h (j t) -> h j t", j=per_head)


def attend(nc, qk_parts, v_all, oT, inverse):
    with ExitStack() as ctx:
        def sb(name, shape, dt=F32):
            return ctx.enter_context(nc.sbuf_tensor(name, shape, dt))

        def sem(name):
            return ctx.enter_context(nc.semaphore("p2_" + name))

        q_st = [sb(f"q_stack{i}", [ROWS, GH, T], BF16) for i in range(SLOTS)]
        k_st = [sb(f"k_stack{i}", [ROWS, GH, T], BF16) for i in range(SLOTS)]
        v_st = [sb(f"v_ones{i}", [P, KT, GH, 2 * HD]) for i in range(SLOTS)]
        prob = [sb(f"prob{i}", [P, GH, CHUNK]) for i in range(P_RING)]
        maxes = sb("maxes", [P, M_MMS // 2, 2])
        maxm = sb("maxm", [P, M_MMS // 2])
        neg = sb("neg_max", [P, 2, M_MMS // 2], BF16)
        negT = [sb(f"neg_maxT{i}", [P, 32], BF16) for i in range(QC)]
        o_sb = [sb(f"o_sb{i}", [P, CHUNK]) for i in range(QC)]
        ps_s = ctx.enter_context(nc.psum_tensor("ps_s", [P, 2, 2, CHUNK], F32))
        ps_m = ctx.enter_context(nc.psum_tensor("ps_m", [P, M_RING, CHUNK], F32))
        ps_o = ctx.enter_context(nc.psum_tensor("ps_o", [P, CHUNK], F32))

        stack_in = [sem(f"stack{i}_loaded") for i in range(SLOTS)]
        ones_set, v_set = sem("ones_set"), sem("v_placed")
        m_ready, m_taken, m_turned = sem("scores_for_max"), sem("max_taken"), sem("max_turned")
        m_in = [sem(f"max_rows_placed{i}") for i in range(QC)]
        m_stored = [sem(f"max_stored{i}") for i in range(QC)]
        neg_rows = nc.dram_tensor("neg_rows", (QC, 32, P), BF16).ap()
        s_ready = sem("scores_for_exp")
        exp_done, pv_done = sem("exp_done"), sem("pv_done")
        o_taken, o_out = sem("o_taken"), [sem(f"o_stored{i}") for i in range(QC)]
        own = sem("vector_steps")
        early = slice(0, B - 1)
        sums, per_head = sb("sums", [2 * H * (B - 1), CHUNK]), 2
        sums_in, inverted, inverse_out = sem("sums_loaded"), sem("inverted"), sem("inverses_stored")
        EXPS, UNITS = 2 * QC * KT, QC * KT
        block = ctx.enter_context(nc.Block())

        @block.sync
        def _(sp):
            def load(g, slot):
                for qk, stack, part in ((0, q_st, Q_PART), (1, k_st, K_PART)):
                    src = qk_parts[qk, bass.ds(g * CG, CG)].rearrange("(h d) a t -> d a h t", d=HD)
                    for i in range(PAIRS):
                        sp.dma_start(stack[slot][i * HD:(i + 1) * HD], src[:, part[i]]).then_inc(stack_in[slot], 16)

            def place_max(g, slot, qc):
                half = QC * g + qc
                sp.wait_ge(m_turned, half + 1)
                sp.dma_start(neg_rows[qc].rearrange("(a b) (c i) -> c (a b) i", a=2, c=4), negT[qc][:]).then_inc(m_stored[qc], 16)
                sp.wait_ge(m_stored[qc], 16 * g + 16)
                sp.dma_start(q_st[slot][MROW:ROWS, :, qc * CHUNK:(qc + 1) * CHUNK],
                             neg_rows[qc].rearrange("(a h t) q -> a h (t q)", a=2, h=GH)).then_inc(m_in[qc], 16)

            def store(g, qc):
                sp.wait_ge(o_taken, QC * g + qc + 1)
                sp.dma_start(oT[bass.ds(g * P, P), qc * CHUNK:(qc + 1) * CHUNK], o_sb[qc][:]).then_inc(o_out[qc], 16)

            def group(g, u, load_ahead=True, first=False, last=False):
                if load_ahead:
                    if not first:
                        sp.wait_ge(exp_done, EXPS * g + 2)
                    load(g + 2, (u + 2) % SLOTS)
                if not first:
                    store(g - 1, 1)
                if not last:
                    place_max(g + 1, (u + 1) % SLOTS, 0)
                if last:
                    sp.wait_ge(inverted, 1)
                    sp.dma_start(inverses_of(inverse, early, per_head), sums[:]).then_inc(inverse_out, 16)
                store(g, 0)
                if not last:
                    place_max(g + 1, (u + 1) % SLOTS, 1)
                else:
                    store(g, 1)

            load(0, 0)
            load(1, 1)
            place_max(0, 0, 0)
            place_max(0, 0, 1)
            for g in range(3):
                group(g, g, first=g == 0)
            with sp.Fori(1, 4) as it:
                for u in range(3):
                    group(3 * it + u, u)
            for g in range(12, NG):
                if g == NG - 3:
                    sp.wait_ge(o_out[0], 16 * g)
                    sp.wait_ge(o_out[1], 16 * (g - 1))
                    sp.dma_start(sums[:], sums_of(oT, early, per_head)).then_inc(sums_in, 16)
                group(g, g % 3, load_ahead=g + 2 < NG, last=g == NG - 1)
            for s in o_out:
                sp.wait_ge(s, 16 * NG)
            sp.wait_ge(inverse_out, 16)

        @block.gpsimd
        def _(pool):
            def place_v(g, slot, first=False):
                if not first:
                    pool.wait_ge(pv_done, UNITS * (g - 2) + 2)
                pool.tensor_copy(v_st[slot][:, :, :, 0:HD],
                                 v_all[:, bass.ds(g, 1)].rearrange("p g k (h d) -> p (g k) h d", d=HD)).then_inc(v_set, 1)

            for i in range(SLOTS):
                pool.memset(v_st[i][:, :, :, HD:], 1.0).then_inc(ones_set, 1)
                place_v(i, i, first=True)
            with pool.Fori(1, 5) as it:
                for u in range(3):
                    place_v(3 * it + u, u)
            place_v(NG - 1, 0)

        @block.scalar
        def _(act):
            act.sem_inc(exp_done, 2)

            def take_o(g, qc):
                act.wait_ge(pv_done, UNITS * g + KT * (qc + 1) + 2)
                act.wait_ge(o_out[qc], 16 * g)
                act.activation(o_sb[qc][:], ps_o[:], ACT.Copy).then_inc(o_taken, 1)

            def group(g, u, first=False):
                for qc in range(QC):
                    for kt in range(KT):
                        n = UNITS * g + KT * qc + kt
                        act.wait_ge(pv_done, n)
                        for pair in range(2):
                            act.wait_ge(s_ready, 2 * n + pair + 1)
                            act.activation(prob[(UNITS * u + KT * qc + kt) % P_RING][:, 2 * pair:2 * pair + 2], ps_s[:, pair],
                                           ACT.Exp, scale=HD ** -0.5).then_inc(exp_done, 1)
                        if kt == 0 and not (first and qc == 0):
                            take_o(g - 1 if qc == 0 else g, 1 - qc)

            for g in range(3):
                group(g, g, first=g == 0)
            with act.Fori(1, 5) as it:
                for u in range(3):
                    group(3 * it + u, u)
            group(NG - 1, 0)
            take_o(NG - 1, 1)

        @block.vector
        def _(dve):
            steps = Steps(dve, own)
            for i in range(SLOTS):
                dve.memset(k_st[i][MROW:ROWS], 1.0).then_inc(ones_set, 1)

            def maxima(g, qc):
                half = QC * g + qc
                steps.at(3 * half)
                for i in range(M_MMS):
                    dve.wait_ge(m_ready, M_MMS * half + i + 1)
                    dve.tensor_reduce(maxes[:, i // 2, i % 2:i % 2 + 1], ps_m[:, (M0 + M_MMS * qc + i) % M_RING],
                                      AX.X, ALU.max).then_inc(m_taken, 1)
                dve.wait_ge(m_taken, M_MMS * (half + 1))
                steps.did(dve.tensor_reduce(maxm[:], maxes[:], AX.X, ALU.max))
                steps.settle()
                steps.did(dve.tensor_scalar(neg[:, 0], maxm[:], -1.0, None, ALU.mult))
                steps.settle()
                steps.did(dve.scalar_tensor_tensor(out=neg[:, 1], in0=maxm[:], scalar=-1.0, in1=neg[:, 0],
                                                   op0=ALU.mult, op1=ALU.subtract))
                steps.settle()
                dve.wait_ge(m_in[qc], 16 * g)
                dve.transpose(negT[qc][:], neg[:].rearrange("p a b -> p (a b)")).then_inc(m_turned, 1)

            M0 = 0
            maxima(0, 0)
            maxima(0, 1)
            for g in range(2):
                M0 = M_MMS * QC * (g + 1)
                maxima(g + 1, 0)
                maxima(g + 1, 1)
            with dve.Fori(1, 5) as it:
                for u in range(3):
                    M0 = M_MMS * QC * u
                    maxima(3 * it + u, 0)
                    maxima(3 * it + u, 1)
            M0 = 0
            maxima(NG - 1, 0)
            maxima(NG - 1, 1)
            dve.wait_ge(sums_in, 16)
            dve.reciprocal(sums[:], sums[:]).then_inc(inverted, 1)

        @block.tensor
        def _(pe):
            pe.sem_inc(pv_done, 2)

            def score_for_max(g, slot, qc, i):
                n = M_MMS * (QC * g + qc) + i
                if not (isinstance(n, int) and n < M_RING):
                    pe.wait_ge(m_taken, n - M_RING + 1)
                h, t, kc = i // 8, i // 2 % 4, i % 2
                q0 = qc * CHUNK + t * P
                pe.matmul(ps_m[:, (M_MMS * (QC * slot + qc) + i) % M_RING], q_st[slot][0:MROW, h, q0:q0 + P],
                          k_st[slot][0:MROW, h, kc * CHUNK:(kc + 1) * CHUNK], start=True, stop=True).then_inc(m_ready, 1)

            def scores(g, slot, qc, kt, pair):
                n = UNITS * g + KT * qc + kt
                pe.wait_ge(exp_done, 2 * n + pair + 1)
                for j in range(2):
                    h = 2 * pair + j
                    ins = pe.matmul(ps_s[:, pair, j], k_st[slot][:, h, kt * P:(kt + 1) * P],
                                    q_st[slot][:, h, qc * CHUNK:(qc + 1) * CHUNK], start=True, stop=True)
                ins.then_inc(s_ready, 1)

            def weigh(g, slot, qc, kt):
                n = UNITS * g + KT * qc + kt
                pe.wait_ge(exp_done, 2 * n + 4)
                if kt == 0:
                    pe.wait_ge(o_taken, QC * g + qc)
                    pe.wait_ge(v_set, g + 1)
                for h in range(GH):
                    ins = pe.matmul(ps_o[32 * h:32 * h + 32], v_st[slot][:, kt, h], prob[(UNITS * slot + KT * qc + kt) % P_RING][:, h],
                                    start=kt == 0, stop=kt == KT - 1)
                ins.then_inc(pv_done, 1)

            def group(g, u, ahead=True, first=False):
                nxt = (u + 1) % SLOTS
                if ahead:
                    pe.wait_ge(stack_in[nxt], 16 * 2 * PAIRS * ((g + 1 - nxt) // 3 + 1))
                for qc in range(QC):
                    pe.wait_ge(m_in[qc], 16 * (g + 1))
                    for kt in range(KT):
                        scores(g, u, qc, kt, 0)
                        if ahead:
                            for i in range(2):
                                score_for_max(g + 1, nxt, qc, 4 * kt + i)
                        scores(g, u, qc, kt, 1)
                        if ahead:
                            for i in range(2, 4):
                                score_for_max(g + 1, nxt, qc, 4 * kt + i)
                        if kt:
                            weigh(g, u, qc, kt - 1)
                        elif qc:
                            weigh(g, u, 0, KT - 1)
                        elif not first:
                            weigh(g - 1, (u - 1) % SLOTS, QC - 1, KT - 1)

            pe.wait_ge(ones_set, 2 * SLOTS)
            pe.wait_ge(stack_in[0], 16 * 2 * PAIRS)
            for qc in range(QC):
                for i in range(M_MMS):
                    score_for_max(0, 0, qc, i)
            for g in range(3):
                group(g, g, first=g == 0)
            with pe.Fori(1, 5) as it:
                for u in range(3):
                    group(3 * it + u, u)
            group(NG - 1, 0, ahead=False)
            weigh(NG - 1, 0, QC - 1, KT - 1)


HALF = 64
LO, HI = slice(0, HALF), slice(HALF, P)
MC = 128
NM = T // MC
SMALL_C, SMALL_E, SMALL_AB, SMALL_F, SMALL_THETA, SMALL_K2 = range(6)
HALO = 3


def mix(nc, const, cols, w, oT, inverse, xres, x2, hidT_out, mem):
    with ExitStack() as ctx:
        def sb(name, shape, dt=F32):
            return ctx.enter_context(nc.sbuf_tensor("p3_" + name, shape, dt))

        def sem(name):
            return ctx.enter_context(nc.semaphore("p3_" + name))

        w_out, w_t, w_p = sb("w_out", [P, CH, C]), const["ternary"], sb("w_p", [P, CH, 3 * P])
        o = [sb(f"o{s}", [P, CH, CHUNK]) for s in range(2)]
        inv = [sb(f"inverse_sums{s}", [P, CH, CHUNK]) for s in range(2)]
        x_in_t, x1_t, x2_t = ([sb(f"{k}{s}", [P, TPC, C]) for s in range(2)] for k in ("x_in", "x1", "x2"))
        z, hid, zT = sb("z", [P, TPC, C]), sb("hid", [P, TPC, C]), sb("zT", [P, CH, CHUNK])
        hT = [sb(f"hT{s}", [P, CH, CHUNK]) for s in range(2)]
        stats, mv, rstd, tmp = sb("stats", [P, 2, TPC, 6]), sb("mv", [P, 2, TPC, 2]), sb("rstd", [P, 2, TPC]), sb("tmp", [P, TPC])
        pre = [[sb(f"pre_{k}{s}", [P, HALO + CHUNK]) for s in range(2)] for k in ("kv", "q")]
        kv_c, q_c = ([sb(f"{k}_c{s}", [P, CHUNK]) for s in range(2)] for k in ("kv", "q"))
        convolutions = ((pre[0], kv_c, COL_KV, slice(0, P)), (pre[1], q_c, COL_Q, LO))
        sig_ea, sig_t, relu_t, soft = (sb(n, [P, CHUNK]) for n in ("sig_ea", "sig_t", "relu_t", "soft"))
        eta, keep = sb("eta", [P, CHUNK]), sb("keep", [P, CHUNK])
        E, fz, kT = sb("E", [P, TPC, MC]), sb("fz", [P, TPC, MC]), sb("kT", [P, TPC, HALF])
        squares = sb("squares", [P, TPC, HALF])
        ab, C_, G, aqb = ([sb(f"{k}{s}", [P, CHUNK]) for s in range(2)] for k in ("ab", "C", "G", "aqb"))
        kce, vT = [sb(f"kce{s}", [P, TPC, P]) for s in range(2)], [sb(f"vT{s}", [P, TPC, HALF]) for s in range(2)]
        small = [sb(f"small{s}", [P, TPC, 6]) for s in range(2)]
        ps_a = ctx.enter_context(nc.psum_tensor("p3_a", [P, 2, 2, C], F32))
        ps_t = ctx.enter_context(nc.psum_tensor("p3_t", [P, CH, CHUNK], F32))
        ps_p = ctx.enter_context(nc.psum_tensor("p3_p", [P, 4, CHUNK], F32))

        w_in, o_in, x_in = sem("weights"), [sem("o0"), sem("o1")], [sem("x0"), sem("x1")]
        o_div, w_ready, var_z, rstd_z, z_ready, zT_turned, zT_ready, f_ready = map(sem, (
            "o_divided", "w_out_in_psum", "var_z", "rstd_z", "z", "zT_in_psum", "zT", "ffn_in_psum"))
        var_h, rstd_h, h_ready, hT_turned, hT_ready = map(sem, ("var_h", "rstd_h", "hid", "hidT_in_psum", "hidT"))
        x2_out, hT_out = [sem("x2_stored0"), sem("x2_stored1")], [sem("hidT_stored0"), sem("hidT_stored1")]
        p_ready, acts, act_own, conv, soft_ready, mean_ready, gate_ready, th_ready, th_taken, kv_ready, kv_taken = map(sem, (
            "projections_in_psum", "projection_banks_read", "activations_steps", "convolved", "softplus", "gate_means_in_psum",
            "gates", "theta_in_psum", "theta_taken", "kvT_in_psum", "kvT_taken"))
        kq_ready, g_ready, scanned, pool_own, fz_set, halo_set, pre_ready = map(sem, (
            "kq_in_psum", "G", "scans", "pool_steps", "zeros_set", "halos_set", "oldest_taps"))
        added_w, added_f, own_z, own_h, own_c, own_s, own_k = map(sem, (
            "added_to_x1", "added_to_x2", "stats_z_steps", "stats_h_steps", "convolution_steps", "scan_steps", "k_norms"))
        late, per_head = slice(B - 1, B), P // H
        late_sums = sb("late_sums", [P, T // per_head])
        sums_moved, inverted = sem("sums_moved"), sem("inverted")
        q_dup = [sem("q_doubled0"), sem("q_doubled1")]
        mem_done = sem("pool_memory_terms")
        ln_ready = sem("ln_ready")
        passed, terms_out, TERMS = sem("passed"), [sem("terms_stored0"), sem("terms_stored1")], 16 * 8
        ROUNDS = NCH // 2
        tok = lambda a: a.rearrange("(n i p) c -> n p i c", i=TPC, p=P)
        block = ctx.enter_context(nc.Block())

        @block.sync
        def _(sp):
            def load(r, s, first=False):
                n = 2 * r + s
                if not first:
                    sp.wait_ge(added_w, 2 * n - 2)
                for c in range(CH):
                    heads = oT[bass.ds((NG // B * r + 2 * c) * P, 2 * P), s * CHUNK:(s + 1) * CHUNK].rearrange(
                        "(h two d) t -> two h d t", two=2, d=HD)[0]
                    sp.dma_start(o[s][:, c], heads).then_inc(o_in[s], 16)
                    sums_c = inverse[bass.ds(H * r + H // CH * c, H // CH), s * CHUNK:(s + 1) * CHUNK]
                    sp.dma_start(inv[s][:, c], sums_c.unsqueeze(1).to_broadcast([H // CH, HD, CHUNK])).then_inc(o_in[s], 16)
                sp.dma_start(x_in_t[s][:], tok(xres)[2 * r + s]).then_inc(x_in[s], 16)

            def store_x2(r, s):
                sp.wait_ge(added_f, 2 * (2 * r + s) + 2)
                sp.dma_start(tok(x2)[2 * r + s], x2_t[s][:]).then_inc(x2_out[s], 16)

            def store_hT(r, s):
                sp.wait_ge(hT_ready, 2 * r + s + 1)
                sp.dma_start(hidT_out[r, :, :, s * CHUNK:(s + 1) * CHUNK], hT[s][:]).then_inc(hT_out[s], 16)

            def store_kv(r, s):
                n = 2 * r + s
                sp.wait_ge(conv, 2 * n + 2)
                sp.dma_start(q_c[s][HI], q_c[s][LO]).then_inc(q_dup[s], 16)
                sp.dma_start(mem["kv"][:, bass.ds(CHUNK * n, CHUNK)], kv_c[s][:]).then_inc(terms_out[s], 16)

            load(0, 0, first=True)
            sp.dma_start(w_out[:], w["w_out"].rearrange("(g p) n -> p g n", p=P)).then_inc(w_in, 16)
            load(0, 1, first=True)
            sp.dma_start(w_p[:], w["w_p"].rearrange("(g p) n -> p g n", p=P)).then_inc(w_in, 16)
            sp.dma_start(late_sums[:], sums_of(oT, late, per_head)).then_inc(sums_moved, 16)
            store_x2(0, 0)
            sp.wait_ge(inverted, 1)
            sp.dma_start(inverses_of(inverse, late, per_head), late_sums[:]).then_inc(sums_moved, 16)
            store_hT(0, 0)
            sp.wait_ge(sums_moved, 32)
            load(1, 0)

            def step(r, s, o_ahead=True):
                if o_ahead:
                    load(r + 1 + s, 1 - s)
                store_x2(r + s, 1 - s)
                store_hT(r + s, 1 - s)
                store_kv(r, s)

            with sp.Fori(0, ROUNDS - 2) as r:
                for s in range(2):
                    step(r, s)
            step(ROUNDS - 2, 0)
            step(ROUNDS - 2, 1, o_ahead=False)
            step(ROUNDS - 1, 0, o_ahead=False)
            store_kv(ROUNDS - 1, 1)
            for s in range(2):
                sp.wait_ge(x2_out[s], 16 * ROUNDS)
                sp.wait_ge(hT_out[s], 16 * ROUNDS)
                sp.wait_ge(terms_out[s], TERMS * ROUNDS)

        @block.gpsimd
        def _(pool):
            steps = Steps(pool, pool_own)
            pool.memset(fz[LO], 0.0).then_inc(fz_set, 1)
            pool.wait_ge(fz_set, 1)

            def deviation(r, s, k, var_ready, ready):
                n = 2 * r + s
                pool.wait_ge(var_ready, n + 1)
                steps.at(2 * n + k)
                inverse_deviation(pool, steps, mv[:, k, :, 1], const, tmp[:], rstd[:, k], ready)

            def divide(r, s):
                pool.wait_ge(o_in[s], 16 * 2 * CH * (r + 1))
                pool.tensor_tensor(o[s][:], o[s][:], inv[s][:], ALU.mult).then_inc(o_div, 1)

            def softplus(r, s, z_ahead, h_ahead):
                n = 2 * r + s
                pool.wait_ge(ln_ready, n + 1)
                pool.wait_ge(th_ready, n)
                pool.wait_ge(mem_done, n)
                pool.wait_ge(rstd_z, n + 1 + z_ahead)
                pool.wait_ge(rstd_h, n + 1 + h_ahead)
                pool.tensor_tensor(soft[HI], relu_t[HI], sig_t[HI], ALU.subtract).then_inc(soft_ready, 1)
                pool.wait_ge(soft_ready, n + 1)

            def memory_terms(r, s):
                n = 2 * r + s
                tiles = bass.ds(TPC * n, TPC)
                pool.wait_ge(scanned, n + 1)
                pool.wait_ge(q_dup[s], 16 * r + 16)
                pool.tensor_tensor(aqb[s][:], ab[s][:], q_c[s][:], ALU.mult)
                pool.wait_ge(kv_taken, n + 1)
                for j in range(2):
                    last = small[s][:, :, j:j + 1].to_broadcast([P, TPC, HALF])
                    ins = pool.tensor_tensor(kce[s][:, :, j * HALF:(j + 1) * HALF], kT[:], last, ALU.mult)
                ins.then_inc(mem_done, 1)

            def step(r, s, z_ahead=2, h_ahead=1, o_ahead=True):
                if z_ahead > 1:
                    deviation(r + 1, s, 0, var_z, rstd_z)
                softplus(r, s, z_ahead, h_ahead)
                if o_ahead:
                    divide(r + 1 + s, 1 - s)
                memory_terms(r, s)
                if z_ahead > 1:
                    deviation(r + 1, s, 1, var_h, rstd_h)

            divide(0, 0)
            divide(0, 1)
            for s in range(2):
                deviation(0, s, 0, var_z, rstd_z)
                deviation(0, s, 1, var_h, rstd_h)
            divide(1, 0)
            with pool.Fori(0, ROUNDS - 2) as r:
                for s in range(2):
                    step(r, s)
            step(ROUNDS - 2, 0)
            step(ROUNDS - 2, 1, o_ahead=False)
            step(ROUNDS - 1, 0, z_ahead=1, o_ahead=False)
            step(ROUNDS - 1, 1, z_ahead=0, h_ahead=0, o_ahead=False)
            pool.wait_ge(mem_done, NCH)

        @block.scalar
        def _(act):
            for before, _, _, part in convolutions:
                act.activation(before[0][part, 0:HALO], cols[part, 0:HALO], ACT.Copy, scale=0.0).then_inc(halo_set, 1)

            def copy_zT(r, s):
                act.wait_ge(zT_turned, 2 * r + s + 1)
                act.activation(zT[:], ps_t[:], ACT.Copy).then_inc(zT_ready, 1)

            def copy_hT(r, s):
                n = 2 * r + s
                act.wait_ge(hT_turned, n + 1)
                act.wait_ge(hT_out[s], 16 * r)
                act.activation(hT[s][:], ps_t[:], ACT.Copy).then_inc(hT_ready, 1)

            def gates(r, s):
                n = 2 * r + s
                theta_b = cols[HI, COL_THETA_B:COL_THETA_B + 1]
                act.wait_ge(soft_ready, n)
                act.wait_ge(terms_out[s], TERMS * r)
                act.wait_ge(p_ready, 3 * n + 1)
                act.activation(pre[0][s][:, HALO:], ps_p[:, 0], ACT.Copy).then_inc(acts, 1)
                act.wait_ge(p_ready, 3 * n + 2)
                act.activation(relu_t[HI], ps_p[HI, 1], ACT.Relu, bias=theta_b)
                act.activation(sig_t[HI], ps_p[HI, 1], ACT.Abs, bias=theta_b).then_inc(act_own, 1)
                act.activation(pre[1][s][LO, HALO:], ps_p[LO, 1], ACT.Copy).then_inc(acts, 1)
                act.wait_ge(p_ready, 3 * n + 3)
                act.activation(sig_ea[:], ps_p[:, 2], ACT.Sigmoid, bias=cols[:, COL_GATE_B:COL_GATE_B + 1]).then_inc(acts, 1)
                act.wait_ge(act_own, 2 * n + 1)
                act.activation(sig_t[HI], sig_t[HI], ACT.Sigmoid).then_inc(act_own, 1)
                act.wait_ge(acts, 3 * n + 2)
                if s:
                    for before, _, _, part in convolutions:
                        act.activation(before[1][part, 0:HALO], before[0][part, CHUNK:], ACT.Copy).then_inc(halo_set, 1)
                act.wait_ge(halo_set, 2 * r + 2 + 2 * s)
                for before, after, col, part in convolutions:
                    act.activation(after[s][part], before[s][part, 0:CHUNK], ACT.Identity, bias=cols[part, col + 4:col + 5],
                                   scale=cols[part, col:col + 1]).then_inc(pre_ready, 1)
                act.wait_ge(act_own, 2 * n + 2)
                act.activation(sig_t[HI], sig_t[HI], ACT.Ln).then_inc(ln_ready, 1)

            def take_means(r, s):
                n = 2 * r + s
                act.wait_ge(scanned, n)
                act.wait_ge(mean_ready, 2 * n + 1)
                act.activation(eta[:], ps_p[:, 0], ACT.Copy, scale=0.9, bias=0.05).then_inc(gate_ready, 1)
                act.wait_ge(mean_ready, 2 * n + 2)
                act.activation(keep[:], ps_p[:, 1], ACT.Copy, scale=-0.1, bias=1.0).then_inc(gate_ready, 1)

            def tails(r, s):
                n = 2 * r + s
                act.wait_ge(kv_ready, n + 1)
                act.wait_ge(mem_done, n)
                act.wait_ge(own_k, TPC * n)
                kv = ps_p[:, 3].rearrange("p (i k d) -> p k i d", k=2, d=HALF)
                act.activation(vT[s][:], kv[:, 1], ACT.Copy)
                act.activation(kT[:], kv[:, 0], ACT.Copy).then_inc(kv_taken, 1)

            def theta(r, s):
                n = 2 * r + s
                act.wait_ge(th_ready, n + 1)
                act.activation(small[s][:, :, SMALL_THETA], ps_p[:, 1, 0:TPC], ACT.Copy, scale=0.02).then_inc(th_taken, 1)

            def store_terms(r, s):
                n = 2 * r + s
                at, tiles = bass.ds(CHUNK * n, CHUNK), bass.ds(TPC * n, TPC)
                act.wait_ge(g_ready, n + 1)
                for name, tile in (("ab", ab), ("C", C_), ("G", G)):
                    act.dma_start(mem[name][:, at], tile[s][:]).then_inc(terms_out[s], 16)
                act.wait_ge(own_k, TPC * n + TPC)
                act.wait_ge(th_taken, n + 1)
                act.dma_start(mem["small"][:, tiles], small[s][:]).then_inc(terms_out[s], 16)
                act.wait_ge(mem_done, n + 1)
                for name, tile in (("vT", vT), ("kce", kce)):
                    act.dma_start(mem[name][:, tiles], tile[s][:]).then_inc(terms_out[s], 16)
                act.dma_start(mem["aqb"][:, at], aqb[s][:]).then_inc(terms_out[s], 16)

            copy_zT(0, 0)
            copy_hT(0, 0)
            copy_zT(0, 1)
            with act.Fori(0, ROUNDS - 1) as r:
                for s in range(2):
                    copy_hT(r + s, 1 - s)
                    gates(r, s)
                    copy_zT(r + 1, s)
                    take_means(r, s)
                    tails(r, s)
                    theta(r, s)
                    store_terms(r, s)
            copy_hT(ROUNDS - 1, 1)
            for s in range(2):
                gates(ROUNDS - 1, s)
                take_means(ROUNDS - 1, s)
                tails(ROUNDS - 1, s)
                theta(ROUNDS - 1, s)
                store_terms(ROUNDS - 1, s)
            act.wait_ge(kv_taken, NCH)

        @block.vector
        def _(dve):
            norm_steps = [Steps(dve, own_z), Steps(dve, own_h)]
            scan_steps = Steps(dve, own_s)

            def norm_z(r, s):
                n = 2 * r + s
                dve.wait_ge(x_in[s], 16 * (r + 1))
                for k in range(2):
                    dve.wait_ge(w_ready, 2 * n + k + 1)
                    dve.tensor_tensor(x1_t[s][:, 2 * k:2 * k + 2], x_in_t[s][:, 2 * k:2 * k + 2], ps_a[:, k], ALU.add).then_inc(added_w, 1)
                dve.wait_ge(added_w, 2 * n + 2)
                norm_steps[0].at(TPC * n)
                moments(dve, norm_steps[0], x1_t[s], stats[:, 0], mv[:, 0], var_z, passed)

            def put_z(r, s):
                n = 2 * r + s
                dve.wait_ge(rstd_z, n + 1)
                dve.wait_ge(zT_turned, n)
                normalise(dve, x1_t[s], mv[:, 0], rstd[:, 0], z, z_ready)

            def norm_h(r, s):
                n = 2 * r + s
                dve.wait_ge(x2_out[s], 16 * r)
                for k in range(2):
                    dve.wait_ge(f_ready, 2 * n + k + 1)
                    dve.tensor_tensor(x2_t[s][:, 2 * k:2 * k + 2], x1_t[s][:, 2 * k:2 * k + 2], ps_a[:, k], ALU.add).then_inc(added_f, 1)
                dve.wait_ge(added_f, 2 * n + 2)
                norm_steps[1].at(TPC * n)
                moments(dve, norm_steps[1], x2_t[s], stats[:, 1], mv[:, 1], var_h, passed)

            def put_h(r, s):
                n = 2 * r + s
                dve.wait_ge(rstd_h, n + 1)
                dve.wait_ge(hT_turned, n)
                normalise(dve, x2_t[s], mv[:, 1], rstd[:, 1], hid, h_ready)

            def convolve(r, s, j):
                n = 2 * r + s
                dve.wait_ge(pre_ready, 2 * n + 2)
                if j > 1:
                    dve.wait_ge(own_c, 4 * n + 2 * (j - 1))
                for before, after, col, part in convolutions:
                    ins = dve.scalar_tensor_tensor(out=after[s][part], in0=before[s][part, j:j + CHUNK], scalar=cols[part, col + j:col + j + 1],
                                                   in1=after[s][part], op0=ALU.mult, op1=ALU.add)
                    if j < HALO:
                        ins.then_inc(own_c, 1)
                    else:
                        ins.then_inc(conv, 1)

            def scans(r, s):
                n = 2 * r + s
                scan_steps.at(2 * n)
                dve.wait_ge(gate_ready, 2 * n + 2)
                dve.wait_ge(mem_done, n)
                for i in range(TPC):
                    c = slice(i * MC, (i + 1) * MC)
                    dve.tensor_tensor_scan(fz[HI, i], eta[HI, c], const["zeros"][HI], 1.0, ALU.mult, ALU.add)
                    ins = dve.tensor_tensor_scan(E[:, i], eta[:, c], const["minus_ident"][:], 0.0, ALU.mult, ALU.add)
                scan_steps.did(ins)
                scan_steps.settle()
                for i in range(TPC):
                    c = slice(i * MC, (i + 1) * MC)
                    dve.tensor_tensor_scan(ab[s][:, c], keep[:, c], fz[:, i], const["ab_init"][:, 0:1],
                                           ALU.mult, ALU.add)
                    ins = dve.tensor_tensor_scan(C_[s][:, c], keep[:, c], E[:, i], 0.0, ALU.mult, ALU.add)
                scan_steps.did(ins)
                scan_steps.settle()
                tiles = bass.ds(TPC * n, TPC)
                c_v = C_[s].rearrange("p (i t) -> p i t", t=MC)
                ab_v = ab[s].rearrange("p (i t) -> p i t", t=MC)
                dve.tensor_copy(small[s][:, :, 0:1], c_v[:, :, MC - 1:])
                dve.tensor_copy(small[s][:, :, 1:2], E[:, :, MC - 1:])
                dve.tensor_copy(small[s][:, :, 2:3], ab_v[:, :, MC - 1:])
                dve.tensor_copy(small[s][:, :, 3:4], fz[:, :, MC - 1:]).then_inc(scanned, 1)

            def products_of_keys(r, s):
                n = 2 * r + s
                dve.wait_ge(kq_ready, n + 1)
                dve.tensor_tensor(G[s][:], ps_p[:, 2], C_[s][:], ALU.mult).then_inc(g_ready, 1)
                dve.wait_ge(kv_taken, n + 1)
                dve.wait_ge(own_k, TPC * n)
                for i in range(TPC):
                    ins = dve.tensor_tensor_reduce(squares[:, i], kT[:, i], kT[:, i], 1.0, 0.0, ALU.mult, ALU.add,
                                                   small[s][:, i, SMALL_K2:SMALL_K2 + 1])
                    ins.then_inc(own_k, 1)

            dve.wait_ge(fz_set, 1)
            dve.wait_ge(halo_set, 2)
            def step(r, s, z_ahead=True, h_ahead=True):
                if h_ahead:
                    put_h(r + s, 1 - s)
                if z_ahead:
                    norm_z(r + 1, s)
                    put_z(r + 1, s)
                for tap in range(1, HALO + 1):
                    convolve(r, s, tap)
                scans(r, s)
                if z_ahead:
                    norm_h(r + 1, s)
                products_of_keys(r, s)

            norm_z(0, 0)
            put_z(0, 0)
            norm_h(0, 0)
            put_h(0, 0)
            dve.wait_ge(sums_moved, 16)
            dve.reciprocal(late_sums[:], late_sums[:]).then_inc(inverted, 1)
            norm_z(0, 1)
            put_z(0, 1)
            norm_h(0, 1)
            with dve.Fori(0, ROUNDS - 1) as r:
                for s in range(2):
                    step(r, s)
            step(ROUNDS - 1, 0, z_ahead=False)
            step(ROUNDS - 1, 1, z_ahead=False, h_ahead=False)
            dve.wait_ge(own_k, TPC * NCH)

        @block.tensor
        def _(pe):
            ident = const["ident"]

            def out_products(r, s):
                n = 2 * r + s
                pe.wait_ge(o_div, n + 1)
                pe.wait_ge(added_f, 2 * n)
                token_products(o[s], w_out, w_ready)

            def token_products(src, weights, done):
                for i in range(TPC):
                    for c in range(CH):
                        ins = pe.matmul(ps_a[:, i // 2, i % 2], src[:, c, i * P:(i + 1) * P], weights[:, c], start=c == 0, stop=c == CH - 1)
                    if i % 2:
                        ins.then_inc(done, 1)

            def turn(src, done):
                for c in range(CH):
                    for i in range(TPC):
                        ins = pe.transpose(ps_t[:, c, i * P:(i + 1) * P], src[:, i, c * P:(c + 1) * P], ident[:])
                ins.then_inc(done, 1)

            def turn_z(r, s):
                n = 2 * r + s
                pe.wait_ge(z_ready, n + 1)
                pe.wait_ge(hT_ready, n)
                turn(z, zT_turned)

            def ffn_products(r, s):
                n = 2 * r + s
                pe.wait_ge(zT_ready, n + 1)
                pe.wait_ge(added_w, 2 * n + 2)
                token_products(zT, w_t, f_ready)

            def turn_h(r, s):
                n = 2 * r + s
                pe.wait_ge(h_ready, n + 1)
                pe.wait_ge(zT_ready, n + 1)
                turn(hid, hT_turned)

            def projections(r, s):
                n = 2 * r + s
                pe.wait_ge(hT_ready, n + 1)
                pe.wait_ge(gate_ready, 2 * n)
                pe.wait_ge(th_taken, n)
                pe.wait_ge(g_ready, n)
                for j in range(3):
                    for c in range(CH):
                        ins = pe.matmul(ps_p[:, j], w_p[:, c, j * P:(j + 1) * P], hT[s][:, c], start=c == 0, stop=c == CH - 1)
                    ins.then_inc(p_ready, 1)

            def gate_means(r, s):
                n = 2 * r + s
                pe.wait_ge(acts, 3 * n + 3)
                for j, part in enumerate((LO, HI)):
                    pe.matmul(ps_p[:, j], const["mean"][part], sig_ea[part], start=True, stop=True).then_inc(mean_ready, 1)

            def memory_products(r, s):
                n = 2 * r + s
                pe.wait_ge(kv_taken, n)
                pe.wait_ge(conv, 2 * n + 2)
                for i in range(TPC):
                    ins = pe.transpose(ps_p[:, 3, i * P:(i + 1) * P], kv_c[s][:, i * P:(i + 1) * P], ident[:])
                ins.then_inc(kv_ready, 1)
                for i in range(TPC):
                    c = slice(i * P, (i + 1) * P)
                    ins = pe.matmul(ps_p[:, 2, c], kv_c[s][LO, c], q_c[s][LO, c], start=True, stop=True)
                ins.then_inc(kq_ready, 1)
                pe.wait_ge(soft_ready, n + 1)
                pe.wait_ge(gate_ready, 2 * n + 2)
                for i in range(TPC):
                    ins = pe.matmul(ps_p[:, 1, i:i + 1], soft[HI, i * P:(i + 1) * P], const["mean"][HI, 0:1], start=True, stop=True)
                ins.then_inc(th_ready, 1)

            def step(r, s, z_ahead=True, h_ahead=True):
                if z_ahead:
                    out_products(r + 1, s)
                if h_ahead:
                    turn_h(r + s, 1 - s)
                projections(r, s)
                if z_ahead:
                    turn_z(r + 1, s)
                gate_means(r, s)
                if z_ahead:
                    ffn_products(r + 1, s)
                memory_products(r, s)

            pe.wait_ge(w_in, 32)
            out_products(0, 0)
            turn_z(0, 0)
            ffn_products(0, 0)
            turn_h(0, 0)
            out_products(0, 1)
            turn_z(0, 1)
            ffn_products(0, 1)
            with pe.Fori(0, ROUNDS - 1) as r:
                for s in range(2):
                    step(r, s)
            step(ROUNDS - 1, 0, z_ahead=False)
            step(ROUNDS - 1, 1, z_ahead=False, h_ahead=False)


def constants(nc, const, cols, rows, w):
    with ExitStack() as ctx:
        def sb(name, shape, dt=F32):
            return ctx.enter_context(nc.sbuf_tensor("p0_" + name, shape, dt))

        sems = []
        ctx.callback(retire, nc, sems)

        def sem(name):
            sems.append(nc.alloc_semaphore("p0_" + name))
            return sems[-1]

        wt, size, small, ones = sb("wt", [P, CH, C]), sb("size", [P, CH, C]), sb("small", [P, 8]), sb("ones", [P, P])
        ps = ctx.enter_context(nc.psum_tensor("p0_ps", [P, 1], F32))
        vec_in, w_in, made, row_sums, total, own = map(sem, ("vectors", "weight", "pool_steps", "row_sums", "total", "vector_steps"))
        block = ctx.enter_context(nc.Block())

        @block.sync
        def _(sp):
            sp.dma_start(wt[:], w["w_ffn"].rearrange("(g p) n -> p g n", p=P)).then_inc(w_in, 16)
            sp.dma_start(cols[:], w["cols"]).then_inc(vec_in, 16)
            sp.dma_start(rows[:].rearrange("p a c -> p (a c)"), w["row_vectors"].to_broadcast([P, 4 * C])).then_inc(vec_in, 16)
            sp.wait_ge(vec_in, 32)

        @block.gpsimd
        def _(pool):
            steps = Steps(pool, made)
            ident, i2 = const["ident"], const["ident2"]
            for tile, value in ((ones, 1.0), (ident, 0.0), (const["minus_ident"], 0.0), (i2, 0.0), (const["zeros"], 0.0), (const["mean"], 1.0 / HALF),
                                (const["ab_init"], 0.0)):
                steps.did(pool.memset(tile[:], value))
            for j, value in enumerate(SCALARS):
                steps.did(pool.memset(const["scalars"][:, j:j + 1], value))
            steps.settle()
            for tile, value in ((ident, 1.0), (const["minus_ident"], -1.0)):
                steps.did(pool.affine_select(out=tile[:], in_=tile[:], compare_op=ALU.not_equal, fill=value, base=0,
                                             pattern=[[-1, P]], channel_multiplier=1))
            for lo in (0, HALF):
                steps.settle()
                part = slice(lo, lo + HALF)
                steps.did(pool.affine_select(out=i2[part], in_=i2[part], compare_op=ALU.not_equal, fill=1.0, base=0,
                                             pattern=[[-1, HALF]], channel_multiplier=1))
            steps.settle()
            steps.did(pool.memset(const["ab_init"][LO], 1.0))
            steps.settle()

        @block.scalar
        def _(act):
            act.wait_ge(w_in, 16)
            act.activation(size[:], wt[:], ACT.Abs, accum_out=small[:, 0:1]).then_inc(row_sums, 1)

        @block.tensor
        def _(pe):
            pe.wait_ge(made, 1)
            pe.wait_ge(row_sums, 1)
            pe.matmul(ps[:], ones[:], small[:, 0:1], start=True, stop=True).then_inc(total, 1)

        @block.vector
        def _(dve):
            steps = Steps(dve, own)
            dve.wait_ge(total, 1)
            steps.did(dve.tensor_scalar(small[:, 1:2], ps[:], 1.0 / (C * C), 1e-5, ALU.mult, ALU.max))
            steps.settle()
            steps.did(dve.tensor_scalar(small[:, 2:3], small[:, 1:2], 0.5, None, ALU.mult))
            steps.did(dve.tensor_scalar(small[:, 3:4], small[:, 1:2], -0.5, None, ALU.mult))
            steps.settle()
            steps.did(dve.tensor_scalar(size[:], wt[:], small[:, 2:3], small[:, 1:2], ALU.is_gt, ALU.mult))
            steps.did(dve.tensor_scalar(const["ternary"][:], wt[:], small[:, 3:4], small[:, 1:2], ALU.is_lt, ALU.mult))
            steps.settle()
            steps.did(dve.tensor_tensor(const["ternary"][:], size[:], const["ternary"][:], ALU.subtract))
            steps.settle()


def remember(nc, const, rows, w, mem, x2, hidT, out):
    with ExitStack() as ctx:
        def sb(name, shape, dt=F32):
            return ctx.enter_context(nc.sbuf_tensor("p4_" + name, shape, dt))

        def sem(name):
            return ctx.enter_context(nc.semaphore("p4_" + name))

        def two(name, shape):
            return [sb(f"{name}{s}", shape) for s in range(2)]

        kv, vT, kce, small = two("kv", [P, B, MC]), two("vT", [P, B, HALF]), two("kce", [P, B, P]), two("small", [P, B, 6])
        aqb, G, C_, ab = two("aqb", [P, B, MC]), two("G", [P, B, MC]), two("C", [P, B, MC]), two("ab", [P, B, MC])
        xr, hT = two("x", [P, B, C]), two("hT", [P, CH, B, P])
        ws1, ws2 = two("ws1", [P, B, P]), two("ws2", [P, B, P])
        aF, g1, g2 = two("aF", [P, B, MC]), two("g1", [P, B, 2, HALF]), two("g2", [P, B, 2, HALF])
        w_gate, w_o, w_t = sb("w_gate", [P, CH, C]), sb("w_o", [HALF, C]), const["ternary"]
        sgF, sgT, aT, ds, u = sb("sgF", [P, B, MC]), sb("sgT", [P, B, HALF]), sb("aT", [P, B, HALF]), sb("ds", [P, B, HALF]), sb("u", [P, B, HALF])
        w2 = sb("w2", [P, B, HALF])
        ace, mixer = sb("ace", [P, B, 2, HALF]), sb("mixer", [P, B, 2, HALF])
        eF, eT, dz = sb("eF", [P, B, MC]), sb("eT", [P, B, HALF]), sb("dz", [P, B, HALF])
        sq, sq_act = sb("sq", [P, B, HALF]), sb("sq_act", [P, 2, B, HALF])
        norms = sb("norms", [P, 8, B])
        sg2, h, hab, G2, rF = sb("sg2", [P, B, MC]), sb("h", [P, B, MC]), sb("hab", [P, B, MC]), sb("G2", [P, B, MC]), sb("rF", [HALF, B, MC])
        gate, gated, z, zT = sb("gate", [P, B, C]), sb("gated", [P, B, C]), sb("z", [P, B, C]), sb("zT", [P, CH, B * P])
        factor = sb("factor", [P, B])
        junk = sb("junk", [P, B, C])
        ms = sb("ms", [P, 4, B])
        stats, mv, rstd, tmp = sb("stats", [P, B, 6]), sb("mv", [P, B, 2]), sb("rstd", [P, B]), sb("tmp", [P, B])
        bank = [ctx.enter_context(nc.psum_tensor(f"p4_bank{i}", [P, CHUNK], F32)) for i in range(4)]
        ps_o = ctx.enter_context(nc.psum_tensor("p4_o", [P, 2, 2, C], F32))
        ps_g = ctx.enter_context(nc.psum_tensor("p4_g", [P, 2, CHUNK], F32))

        def cols(b, n):
            return slice(b * n, (b + 1) * n)

        w_in, set0 = sem("weights_loaded"), sem("states_zeroed")
        chain_in, out_in, x_in = ([sem(f"{k}{s}") for s in range(2)] for k in ("chain_terms", "output_terms", "x2_loaded"))
        z_ready, sg_ready, aF_ready, aT_ready = map(sem, ("z1_in_psum", "sigmoids_and_w2", "aF", "aT"))
        p_ready, e_ready, da_ready, pool_ready = map(sem, ("predictions_in_psum", "eF_and_eT", "da_in_psum", "mixer_slope_ace"))
        squares_a, squares_e, norm_ready, pow_ready, g_ready, st_ready, ws_ready = map(sem, (
            "a_norms", "e_norms", "gradient_norms", "inverse_norms", "gradients", "states_in_psum", "states"))
        z2_ready, sg2_ready, h_ready, ah_ready, G2_ready, hab_ready, r_ready, rF_ready = map(sem, (
            "z2_in_psum", "sigmoid_2", "h", "ah_in_psum", "G2", "h_scaled", "r_in_psum", "rF"))
        gate_ready, o_ready, ms_ready, rms_ready, gate_taken, gated_ready, x3_ready = map(sem, (
            "gate_in_psum", "out_in_psum", "mean_squares", "inverse_rms", "gate", "gate_normed", "x3"))
        y_ready, var_ready, rstd_ready, zn_ready, zT_turned, zT_ready, f_ready, x4_ready, x4_out = map(sem, (
            "y", "variance", "rstd", "z", "zT_in_psum", "zT", "ffn_in_psum", "x4", "x4_stored"))
        da_taken, passed = sem("da_taken"), sem("passed")
        NORM_STEPS, WEIGHTS = B + 4, 16 * 4
        own_n, own_s, own_p, own_a = map(sem, ("norm_steps", "stats_steps", "pool_steps", "pool_slope_steps"))
        passed_dve = sem("passed_dve")
        tok = lambda a: a.rearrange("(b c p) n -> c p b n", b=B, p=P)
        x2_c, out_c, hT_c = tok(x2), tok(out), hidT.rearrange("b p g (c t) -> c p g b t", t=MC)

        def terms(name, c):
            m = mem[name]
            if len(m.shape) == 3:
                m = m.rearrange("p (b c) n -> p c b n", b=B)
            else:
                m = m.rearrange("p (b c n) -> p c b n", b=B, c=NM)
            return m[:, bass.ds(c, 1)].rearrange("p o b n -> p (o b) n")

        block = ctx.enter_context(nc.Block())

        @block.sync
        def _(sp):
            def load_chain(c, s):
                if not (isinstance(c, int) and c < 2):
                    sp.wait_ge(ws_ready, 2 * (c - 1))
                for dst, name in ((kv[s][:], "kv"), (vT[s][:], "vT"), (kce[s][:], "kce"), (small[s][:], "small")):
                    sp.dma_start(dst, terms(name, c)).then_inc(chain_in[s], 16)

            def load_out(c, s):
                if not (isinstance(c, int) and c < 2):
                    sp.wait_ge(r_ready, c - 1)
                for dst, name in ((aqb, "aqb"), (G, "G"), (C_, "C"), (ab, "ab")):
                    sp.dma_start(dst[s][:], terms(name, c)).then_inc(out_in[s], 16)
                for g in range(CH):
                    sp.dma_start(hT[s][:, g], hT_c[c][:, g]).then_inc(out_in[s], 16)

            def load_x(c, s):
                if not (isinstance(c, int) and c < 2):
                    sp.wait_ge(x4_out, 16 * (c - 1))
                sp.dma_start(xr[s][:], x2_c[c]).then_inc(x_in[s], 16)

            def store(c, s):
                sp.wait_ge(x4_ready, 2 * c + 2)
                sp.dma_start(out_c[c], xr[s][:]).then_inc(x4_out, 16)

            for tile, name in ((ws1, "m1T"), (ws2, "m2T")):
                sp.dma_start(tile[0][LO].rearrange("p b (j n) -> p (b j) n", j=2),
                             w[name].unsqueeze(1).to_broadcast([HALF, 2 * B, HALF])).then_inc(w_in, 16)
            load_chain(0, 0)
            sp.dma_start(w_gate[:], w["w_gate"].rearrange("(g p) n -> p g n", p=P)).then_inc(w_in, 16)
            sp.dma_start(w_o[:], w["w_o"]).then_inc(w_in, 16)
            load_chain(1, 1)
            load_out(0, 0)

            def step(c, s):
                if not (isinstance(c, int) and c == NM - 1):
                    load_chain(c + 1, 1 - s)
                load_out(c, s)
                load_x(c - 1, 1 - s)
                if not (isinstance(c, int) and c < 2):
                    store(c - 2, s)

            step(1, 1)
            with sp.Fori(1, NM // 2 - 1) as r:
                for s in range(2):
                    step(2 * r + s, s)
            step(NM - 2, 0)
            step(NM - 1, 1)
            load_x(NM - 1, 1)
            store(NM - 2, 0)
            store(NM - 1, 1)
            sp.wait_ge(x4_out, 16 * NM)

        @block.tensor
        def _(pe):
            ident = const["ident"]

            def each(fn, done):
                for b in range(B):
                    ins = fn(b)
                ins.then_inc(done, 1)

            def c1(c, s):
                pe.wait_ge(chain_in[s], 16 * 4 * ((c - s) // 2 + 1))
                pe.wait_ge(ws_ready, 2 * c)
                pe.sem_inc(passed, 1)
                each(lambda b: pe.matmul(bank[0][LO, cols(b, MC)], ws1[s][LO, b, 0:HALF], kv[s][LO, b], start=True, stop=True), z_ready)
                pe.wait_ge(norm_ready, c)
                each(lambda b: pe.matmul(bank[1][:, cols(b, HALF)], kv[s][LO, b], ws1[s][LO, b, 0:HALF], start=True, stop=True), z_ready)
                each(lambda b: pe.transpose(bank[2][:, cols(b, HALF)], ws2[s][LO, b], ident[LO, 0:HALF]), z_ready)

            def c2(c, s):
                pe.wait_ge(aF_ready, c + 1)
                pe.sem_inc(passed, 1)
                each(lambda b: pe.matmul(bank[0][HI, cols(b, MC)], ws2[s][LO, b, 0:HALF], aF[s][LO, b], start=True, stop=True), p_ready)
                pe.wait_ge(aT_ready, c + 1)
                each(lambda b: pe.matmul(bank[1][:, cols(b, HALF)], aF[s][LO, b], ws2[s][LO, b, 0:HALF], start=True, stop=True), p_ready)

            def c3(c, s):
                pe.wait_ge(sg_ready, 3 * c + 3)
                pe.wait_ge(e_ready, 2 * c + 2)
                each(lambda b: pe.matmul(bank[1][:, cols(b, HALF)], eF[HI, b], w2[HI, b], start=True, stop=True), da_ready)

            def c4(c, s):
                pe.wait_ge(pool_ready, 3 * c + 3)
                pe.wait_ge(g_ready, 2 * c + 2)
                for j, (lhs, grad, state) in enumerate(((kce[s], g1[s], ws1[s]), (ace, g2[s], ws2[s]))):
                    for b in range(B):
                        o_b = bank[2 * j][:, cols(b, P)]
                        lhs_b = lhs[:, b] if j == 0 else lhs[:, b].rearrange("p a n -> p (a n)")
                        pe.matmul(o_b, lhs_b, grad[:, b].rearrange("p a n -> p (a n)"), start=True, stop=False)
                        ins = pe.matmul(o_b, mixer[:, b].rearrange("p a n -> p (a n)"), state[:, b], start=False, stop=True)
                    ins.then_inc(st_ready, 1)

            def o1(c, s):
                pe.wait_ge(out_in[s], 16 * 6 * ((c - s) // 2 + 1))
                pe.wait_ge(rF_ready, c)
                for b in range(B):
                    o_b = bank[3][:, cols(b, MC)]
                    pe.matmul(o_b, g1[s][:, b].rearrange("p a n -> p (a n)"), G[s][:, b], start=True, stop=False)
                    ins = pe.matmul(o_b, ws1[s][:, b], aqb[s][:, b], start=False, stop=True)
                ins.then_inc(z2_ready, 1)

            def o2(c, s):
                pe.wait_ge(h_ready, c + 1)
                each(lambda b: pe.matmul(bank[3][:, cols(b, MC)], aF[s][LO, b], h[LO, b], start=True, stop=True), ah_ready)

            def gates(c, s):
                if not (isinstance(c, int) and c < 1):
                    pe.wait_ge(x4_ready, 2 * c - 2)
                for b in range(B):
                    for g in range(CH):
                        ins = pe.matmul(ps_g[:, b // 2, cols(b % 2, C)], hT[s][:, g, b], w_gate[:, g], start=g == 0, stop=g == CH - 1)
                ins.then_inc(gate_ready, 1)

            def o3(c, s):
                pe.wait_ge(G2_ready, c + 1)
                pe.wait_ge(hab_ready, c + 1)
                for b in range(B):
                    o_b = bank[3][LO, cols(b, MC)]
                    pe.matmul(o_b, g2[s][:, b, 0], G2[:, b], start=True, stop=False)
                    ins = pe.matmul(o_b, ws2[s][:, b, 0:HALF], hab[:, b], start=False, stop=True)
                ins.then_inc(r_ready, 1)

            def o4(c, s):
                pe.wait_ge(rF_ready, c + 1)
                pe.wait_ge(y_ready, c)
                each(lambda b: pe.matmul(ps_o[:, b // 2, b % 2], rF[:, b], w_o[:], start=True, stop=True), o_ready)

            def turn(c, s):
                pe.wait_ge(zn_ready, c + 1)
                pe.wait_ge(gate_taken, min(c + 2, NM) if isinstance(c, int) else c + 2)
                for g in range(CH):
                    for b in range(B):
                        ins = pe.transpose(ps_g[:, g, cols(b, P)], z[:, b, g * P:(g + 1) * P], ident[:])
                ins.then_inc(zT_turned, 1)

            def ffn(c, s):
                pe.wait_ge(zT_ready, c + 1)
                for b in range(B):
                    for g in range(CH):
                        ins = pe.matmul(ps_g[:, b // 2, cols(b % 2, C)], zT[:, g, cols(b, P)], w_t[:, g], start=g == 0, stop=g == CH - 1)
                    if b % 2:
                        ins.then_inc(f_ready, 1)

            def step(c, s, stages=3, first=0):
                chain, outputs, ending = (first <= i < stages for i in range(3))
                t = 1 - s
                if chain:
                    c1(c, s)
                if outputs:
                    o1(c - 1, t)
                if chain:
                    c2(c, s)
                if outputs:
                    o2(c - 1, t)
                if chain:
                    c3(c, s)
                if outputs:
                    gates(c - 1, t)
                    o3(c - 1, t)
                if chain:
                    c4(c, s)
                if ending:
                    turn(c - 2, s)
                if outputs:
                    o4(c - 1, t)
                if ending:
                    ffn(c - 2, s)

            pe.wait_ge(w_in, WEIGHTS)
            pe.wait_ge(set0, 2)
            step(0, 0, 1)
            step(1, 1, 2)
            with pe.Fori(1, NM // 2) as r:
                for s in range(2):
                    step(2 * r + s, s)
            step(NM, 0, 3, first=1)
            step(NM + 1, 1, 3, first=2)

        @block.scalar
        def _(act):
            def c1(c, s):
                act.wait_ge(z_ready, 3 * c + 1)
                act.activation(sgF[LO], bank[0][LO].rearrange("p (b n) -> p b n", b=B), ACT.Sigmoid).then_inc(sg_ready, 1)
                act.wait_ge(z_ready, 3 * c + 2)
                act.activation(sgT[:], bank[1][:, 0:B * HALF].rearrange("p (b n) -> p b n", b=B), ACT.Sigmoid).then_inc(sg_ready, 1)
                act.wait_ge(z_ready, 3 * c + 3)
                act.activation(w2[HI], bank[2][HI, 0:B * HALF].rearrange("p (b n) -> p b n", b=B), ACT.Copy).then_inc(sg_ready, 1)

            def squares(src, j, ready, count, done):
                act.wait_ge(ready, count)
                for b in range(B):
                    act.activation(sq_act[:, j, b], src[:, b], ACT.Square, accum_out=norms[:, j, b:b + 1]).then_inc(done, 1)

            def c4(c, s):
                for j, state in enumerate((ws1, ws2)):
                    act.wait_ge(st_ready, 2 * c + j + 1)
                    act.activation(state[1 - s][:], bank[2 * j].rearrange("p (b n) -> p b n", b=B), ACT.Copy).then_inc(ws_ready, 1)

            def sigmoid2(c):
                act.wait_ge(z2_ready, c + 1)
                act.activation(sg2[:], bank[3].rearrange("p (b n) -> p b n", b=B), ACT.Sigmoid).then_inc(sg2_ready, 1)

            def r_out(c):
                act.wait_ge(r_ready, c + 1)
                act.activation(rF[:], bank[3][LO].rearrange("p (b n) -> p b n", b=B), ACT.Copy).then_inc(rF_ready, 1)

            def mean_squares(c):
                act.wait_ge(o_ready, c + 1)
                act.wait_ge(ms_ready, B * c)
                for b in range(B):
                    act.activation(junk[:, b], ps_o[:, b // 2, b % 2], ACT.Square, scale=C ** -0.5,
                                   accum_out=ms[:, 0, b:b + 1]).then_inc(ms_ready, 1)

            def copy_zT(c):
                act.wait_ge(zT_turned, c + 1)
                act.activation(zT[:], ps_g[:], ACT.Copy).then_inc(zT_ready, 1)

            def step(c, s, stages=3, first=0):
                chain, outputs, ending = (first <= i < stages for i in range(3))
                t = 1 - s
                if chain:
                    c1(c, s)
                if outputs:
                    sigmoid2(c - 1)
                if chain:
                    squares(aT, 0, aT_ready, c + 1, squares_a)
                    squares(eT, 1, e_ready, 2 * c + 2, squares_e)
                if outputs:
                    r_out(c - 1)
                if chain:
                    c4(c, s)
                if ending:
                    copy_zT(c - 2)
                if outputs:
                    mean_squares(c - 1)

            step(0, 0, 1)
            step(1, 1, 2)
            with act.Fori(1, NM // 2) as r:
                for s in range(2):
                    step(2 * r + s, s)
            step(NM, 0, 3, first=1)
            step(NM + 1, 1, 3, first=2)
            act.wait_ge(ws_ready, 2 * NM)

        @block.gpsimd
        def _(pool):
            def wide(ap):
                return ap.to_broadcast([P, B, HALF])

            def c1(c, s):
                pool.wait_ge(chain_in[s], 16 * 4 * ((c - s) // 2 + 1))
                pool.wait_ge(ws_ready, 2 * c)
                ident2 = const["ident2"][:].unsqueeze(1).to_broadcast([P, B, HALF])
                for j in range(2):
                    ins = pool.tensor_tensor(mixer[:, :, j], ident2, wide(small[s][:, :, 2 + j:3 + j]), ALU.mult)
                ins.then_inc(pool_ready, 1)
                pool.wait_ge(sg_ready, 3 * c + 2)
                pool.tensor_tensor(u[:], sgT[:], scalar(const, S_ONE, u.shape), ALU.subtract).then_inc(own_a, 1)
                pool.wait_ge(own_a, 2 * c + 1)
                pool.wait_ge(aT_ready, c + 1)
                pool.tensor_tensor(u[:], u[:], aT[:], ALU.mult).then_inc(own_a, 1)
                pool.wait_ge(own_a, 2 * c + 2)
                pool.wait_ge(da_taken, c)
                pool.tensor_tensor(ds[:], sgT[:], u[:], ALU.subtract).then_inc(pool_ready, 1)
                for j in range(2):
                    ins = pool.tensor_tensor(ace[:, :, j], aT[:], wide(small[s][:, :, j:j + 1]), ALU.mult)
                ins.then_inc(pool_ready, 1)

            def power(src, dst, done):
                pool.tensor_tensor(dst, src, scalar(const, S_MINUS_HALF, [P, B]), ALU.pow).then_inc(done, 1)

            def scale_h(c, s):
                pool.wait_ge(h_ready, c + 1)
                pool.wait_ge(r_ready, c)
                pool.tensor_tensor(hab[:], h[:], ab[s][:], ALU.mult).then_inc(hab_ready, 1)

            def c4(c):
                pool.wait_ge(norm_ready, c + 1)
                power(norms[:, 6], norms[:, 7], pow_ready)

            def inverse_rms(c):
                pool.wait_ge(ms_ready, B * (c + 1))
                pool.tensor_tensor(ms[:, 1], ms[:, 0], scalar(const, S_RMS_EPS, [P, B]), ALU.add).then_inc(own_p, 1)
                pool.wait_ge(own_p, 2 * c + 1)
                power(ms[:, 1], ms[:, 2], rms_ready)

            def norm_gate(c):
                pool.wait_ge(gate_taken, c + 1)
                pool.wait_ge(y_ready, c)
                pool.tensor_tensor(gated[:], gate[:], rows[:, ROW_NORMG:ROW_NORMG + 1].to_broadcast([P, B, C]), ALU.mult).then_inc(gated_ready, 1)

            def deviation(c):
                pool.wait_ge(var_ready, c + 1)
                steps = Steps(pool, own_p)
                steps.at(2 * c + 1)
                inverse_deviation(pool, steps, mv[:, :, 1], const, tmp[:], rstd[:], rstd_ready)

            def step(c, s, stages=3, first=0):
                chain, outputs, ending = (first <= i < stages for i in range(3))
                t = 1 - s
                if chain:
                    c1(c, s)
                if outputs:
                    scale_h(c - 1, t)
                if chain:
                    c4(c)
                if ending:
                    deviation(c - 2)
                if outputs:
                    norm_gate(c - 1)
                    inverse_rms(c - 1)

            step(0, 0, 1)
            step(1, 1, 2)
            with pool.Fori(1, NM // 2) as r:
                for s in range(2):
                    step(2 * r + s, s)
            step(NM, 0, 3, first=1)
            step(NM + 1, 1, 3, first=2)

        @block.vector
        def _(dve):
            dve.memset(ws1[0][HI], 0.0).then_inc(set0, 1)
            dve.memset(ws2[0][HI], 0.0).then_inc(set0, 1)
            norm_steps, stat_steps = Steps(dve, own_n), Steps(dve, own_s)

            def split(ap, n=B):
                return ap.rearrange("p (b n) -> p b n", b=n)

            def c1(c, s):
                dve.wait_ge(sg_ready, 3 * c + 1)
                dve.tensor_tensor(aF[s][LO], split(bank[0][LO]), sgF[LO], ALU.mult).then_inc(aF_ready, 1)
                dve.wait_ge(sg_ready, 3 * c + 2)
                dve.wait_ge(pool_ready, 3 * c)
                dve.wait_ge(squares_a, B * c)
                dve.tensor_tensor(aT[:], split(bank[1][:, 0:B * HALF]), sgT[:], ALU.mult).then_inc(aT_ready, 1)

            def c2(c, s):
                dve.wait_ge(p_ready, 2 * c + 1)
                dve.tensor_tensor(eF[HI], split(bank[0][HI]), kv[s][HI], ALU.subtract).then_inc(e_ready, 1)
                dve.wait_ge(p_ready, 2 * c + 2)
                dve.wait_ge(squares_e, B * c)
                dve.tensor_tensor(eT[:], split(bank[1][:, 0:B * HALF]), vT[s][:], ALU.subtract).then_inc(e_ready, 1)

            def c3(c, s, ending):
                dve.wait_ge(da_ready, c + 1)
                dve.wait_ge(pool_ready, 3 * c + 2)
                norm_steps.at(NORM_STEPS * c)
                dve.tensor_tensor(dz[:], split(bank[1][:, 0:B * HALF]), ds[:], ALU.mult).then_inc(da_taken, 1)
                dve.wait_ge(da_taken, c + 1)
                dve.wait_ge(squares_a, B * (c + 1))
                dve.wait_ge(squares_e, B * (c + 1))
                norm_steps.did(dve.tensor_tensor(norms[:, 3], norms[:, 0], norms[:, 1], ALU.mult))
                for b in range(B):
                    norm_steps.did(dve.tensor_tensor_reduce(sq[:, b], dz[:, b], dz[:, b], 1.0, 0.0, ALU.mult, ALU.add, norms[:, 2, b:b + 1]))
                norm_steps.settle()
                norm_steps.did(dve.tensor_tensor(norms[:, 4], norms[:, 2], small[s][:, :, 5], ALU.mult))
                norm_steps.settle()
                norm_steps.did(dve.tensor_tensor(norms[:, 5], norms[:, 3], norms[:, 4], ALU.add))
                norm_steps.settle()
                dve.tensor_scalar(norms[:, 6], norms[:, 5], 0.04, RMS_EPS ** 2, ALU.mult, ALU.max).then_inc(norm_ready, 1)
                if ending:
                    add_output(c - 2, s)
                dve.wait_ge(pow_ready, c + 1)
                norm_steps.did(dve.scalar_tensor_tensor(out=factor[:], in0=norms[:, 7], scalar=1.0, in1=small[s][:, :, 4], op0=ALU.min, op1=ALU.mult))
                norm_steps.settle()
                for src, dst in ((dz, g1), (eT, g2)):
                    dve.tensor_tensor(dst[s][:], src[:].unsqueeze(2).to_broadcast([P, B, 2, HALF]),
                                      factor[:].unsqueeze(2).unsqueeze(3).to_broadcast([P, B, 2, HALF]), ALU.mult).then_inc(g_ready, 1)

            def o1(c, s):
                dve.wait_ge(sg2_ready, c + 1)
                dve.wait_ge(hab_ready, c)
                dve.tensor_tensor(h[:], split(bank[3][:]), sg2[:], ALU.mult).then_inc(h_ready, 1)

            def o2(c, s):
                dve.wait_ge(ah_ready, c + 1)
                dve.tensor_tensor(G2[:], split(bank[3][:]), C_[s][:], ALU.mult).then_inc(G2_ready, 1)

            def take_gate(c):
                dve.wait_ge(gate_ready, c + 1)
                dve.wait_ge(gated_ready, c)
                dve.tensor_tensor(gate[:], ps_g.rearrange("p a (k n) -> p (a k) n", n=C), rows[:, ROW_GB:ROW_GB + 1].to_broadcast([P, B, C]),
                                  ALU.add).then_inc(gate_taken, 1)

            def combine(c, s):
                dve.wait_ge(rms_ready, c + 1)
                dve.wait_ge(gated_ready, c + 1)
                stat_steps.at((2 * B) * c)
                for b in range(B):
                    stat_steps.did(dve.scalar_tensor_tensor(out=gated[:, b], in0=ps_o[:, b // 2, b % 2], scalar=ms[:, 2, b:b + 1], in1=gated[:, b],
                                                            op0=ALU.mult, op1=ALU.mult))

            def add_output(c, s):
                stat_steps.at(2 * B * c + B)
                stat_steps.settle()
                dve.wait_ge(x_in[s], 16 * ((c - s) // 2 + 1))
                dve.tensor_tensor(xr[s][:], xr[s][:], gated[:], ALU.add).then_inc(y_ready, 1)

            def statistics(c, s):
                stat_steps.at(2 * B * c + B)
                dve.wait_ge(y_ready, c + 1)
                moments(dve, stat_steps, xr[s], stats, mv, var_ready, passed_dve)

            def finish(c, s):
                dve.wait_ge(rstd_ready, c + 1)
                dve.wait_ge(zT_turned, c)
                normalise(dve, xr[s], mv, rstd, z, zn_ready)

            def add_ffn(c, s):
                for k in range(2):
                    dve.wait_ge(f_ready, 2 * c + k + 1)
                    x_k = xr[s][:, 2 * k:2 * k + 2]
                    dve.tensor_tensor(x_k, x_k, ps_g[:, k].rearrange("p (a n) -> p a n", a=2), ALU.add).then_inc(x4_ready, 1)

            def step(c, s, stages=3, first=0):
                chain, outputs, ending = (first <= i < stages for i in range(3))
                t = 1 - s
                if chain:
                    c1(c, s)
                if ending:
                    combine(c - 2, s)
                if outputs:
                    o1(c - 1, t)
                if chain:
                    c2(c, s)
                if outputs:
                    o2(c - 1, t)
                if chain:
                    c3(c, s, ending)
                elif ending:
                    add_output(c - 2, s)
                if ending:
                    statistics(c - 2, s)
                if outputs:
                    take_gate(c - 1)
                if ending:
                    finish(c - 2, s)
                    add_ffn(c - 2, s)

            step(0, 0, 1)
            step(1, 1, 2)
            with dve.Fori(1, NM // 2) as r:
                for s in range(2):
                    step(2 * r + s, s)
            step(NM, 0, 3, first=1)
            step(NM + 1, 1, 3, first=2)


_INS = ["x", "w_qkv", "cols", "row_vectors", "w_ffn", "w_out", "w_p", "w_gate", "w_o", "m1T", "m2T"]


def build(nc, t, out):
    with ExitStack() as ctx:
        def sb(name, shape, dt=F32):
            return ctx.enter_context(nc.sbuf_tensor(name, shape, dt))

        def dram(name, shape, dt=F32):
            return nc.dram_tensor(name, shape, dt).ap()

        cols, rows = sb("cols", [P, NCOLS]), sb("rows", [P, 4, C])
        const = {"ident": sb("ident", [P, P]), "minus_ident": sb("minus_ident", [P, P]), "ident2": sb("ident2", [P, HALF]),
                 "zeros": sb("zeros", [P, MC]), "mean": sb("mean", [P, P]), "scalars": sb("scalars", [P, len(SCALARS)]),
                 "ab_init": sb("ab_init", [P, 1]), "ternary": sb("ternary", [P, CH, C])}
        qk_parts = dram("qk_parts", (2, B * C, PARTS, T), BF16)
        xres, x2 = dram("xres", (TOK, C)), dram("x2", (TOK, C))
        oT, inverse = dram("oT", (NG * P, T)), dram("inverse_sums", (B * H, T))
        hidT = dram("hidT", (B, P, CH, T))

        constants(nc, const, cols, rows, t)
        with ExitStack() as attention:
            v_all = attention.enter_context(nc.sbuf_tensor("v_all", [P, NG, KT, CG], F32))
            project(nc, t["x"], t["w_qkv"], cols, rows, const, qk_parts, v_all, xres)
            attend(nc, qk_parts, v_all, oT, inverse)
        mem = {"kv": dram("m_kv", (P, TOK)), "aqb": dram("m_aqb", (P, TOK)), "C": dram("m_C", (P, TOK)), "G": dram("m_G", (P, TOK)),
               "ab": dram("m_ab", (P, TOK)), "kce": dram("m_kce", (P, NT, P)), "vT": dram("m_vT", (P, NT, HALF)), "small": dram("m_small", (P, NT, 6))}
        mix(nc, const, cols, t, oT, inverse, xres, x2, hidT, mem)
        remember(nc, const, rows, t, mem, x2, hidT, out.rearrange("b t c -> (b t) c"))


_OUTS = [((B, T, C), "float32")]


def lay_out(inp):
    attn = lambda n: inp["L0_attn_a_" + n]
    memo = lambda n: inp["L0_attn_b_" + n]
    a = {"x": attn("x").reshape(TOK, C), "w_qkv": attn("w_qkv"), "w_out": attn("w_out"),
         "w_ffn": inp["L0_ffn_weight"].T, "w_gate": memo("gW").T, "w_o": memo("Wo").T, "m1T": memo("mW1").T, "m2T": memo("mW2").T,
         "w_p": np.concatenate([memo(n) for n in ("Wk", "Wv", "Wq", "tW", "eW", "aW")]).T}
    cols = np.zeros((P, NCOLS), np.float32)
    for v, at in ((attn("ln_gamma"), COL_GAMMA), (attn("ln_beta"), COL_BETA), (attn("b_qkv")[:2 * C], COL_BQK)):
        cols[:, at:at + v.size // P] = v.reshape(-1, P).T
    for part, at, n in ((LO, COL_KV, "ck"), (HI, COL_KV, "cv"), (LO, COL_Q, "cq")):
        cols[part, at:at + 4] = memo(n + "w")
        cols[part, at + 4] = memo(n + "b")
    for part, at, n in ((LO, COL_GATE_B, "eb"), (HI, COL_GATE_B, "ab"), (HI, COL_THETA_B, "tb")):
        cols[part, at] = memo(n)
    a["cols"] = cols
    a["row_vectors"] = np.concatenate([attn("b_qkv")[2 * C:], attn("b_out"), memo("norm_g"), memo("gb")]).reshape(1, 4 * C)
    return {k: np.ascontiguousarray(v) for k, v in a.items()}


def kernel(**inputs):
    import numpy as _np
    import concourse.bacc as _bacc
    from concourse import mybir as _mybir
    from concourse.bass_utils import run_bass_kernel_spmd as _run

    nc = _bacc.Bacc("TRN2", target_bir_lowering=False, num_devices=1)
    laid = lay_out({name: _np.asarray(a) for name, a in inputs.items()})
    arrays = {f"in_{name}_dram": laid[name] for name in _INS}
    t = {name: nc.dram_tensor(f"in_{name}_dram", laid[name].shape, _mybir.dt.from_np(laid[name].dtype), kind="ExternalInput").ap()
         for name in _INS}
    shape, dtype = _OUTS[0]
    out = nc.dram_tensor("out_0_dram", shape, _mybir.dt.from_np(_np.dtype(dtype)), kind="ExternalOutput").ap()
    build(nc, t, out)
    r = _run(nc, [arrays], core_ids=[0])
    return r.results[0]["out_0_dram"]
```
